# Optimizing a Trainium2 kernel written in Bass

```python
import numpy as np
import jax
import jax.numpy as jnp

def _softmax(x, axis=-1):
    return jax.nn.softmax(x, axis=axis)

def _gelu(x):
    return jax.nn.gelu(x, approximate=True)

def _silu(x):
    return jax.nn.silu(x)

def _sigmoid(x):
    return jax.nn.sigmoid(x)

def _layernorm(x, axis=-1, eps=1e-05):
    m = jnp.mean(x, axis=axis, keepdims=True)
    v = jnp.var(x, axis=axis, keepdims=True)
    return (x - m) / jnp.sqrt(v + eps)

def _scatter_add(tgt, idx, src, axis=0):
    return tgt.at[idx].add(src)

def _segment_sum(src, seg, n):
    return jax.ops.segment_sum(src, seg, n)
kernel_name = 'mk_recurrent_d1_jaxref_r2_9564ea'

def setup_inputs(seed: int=0):
    np.random.seed(seed)
    _w = jnp.asarray

    def _L0_attn_setup():
        import jax, jax.numpy as jnp
        import numpy as np
        D_MODEL = 1024
        N_HEADS = 16
        HEAD_DIM = D_MODEL // N_HEADS
        SCALE = HEAD_DIM ** (-0.5)
        key = jax.random.key(seed)
        ks = jax.random.split(key, 9)
        B, L, D = (4, 2048, D_MODEL)
        s = 1.0 / np.sqrt(D)
        inp = {'x': jax.random.normal(ks[0], (B, L, D), dtype=jnp.float32)}
        inp['Wq'] = jax.random.normal(ks[1], (D, D), dtype=jnp.float32) * s
        inp['bq'] = jnp.zeros((D,), dtype=jnp.float32)
        inp['Wk'] = jax.random.normal(ks[2], (D, D), dtype=jnp.float32) * s
        inp['bk'] = jnp.zeros((D,), dtype=jnp.float32)
        inp['Wv'] = jax.random.normal(ks[3], (D, D), dtype=jnp.float32) * s
        inp['bv'] = jnp.zeros((D,), dtype=jnp.float32)
        inp['Wo'] = jax.random.normal(ks[4], (D, D), dtype=jnp.float32) * s
        inp['bo'] = jnp.zeros((D,), dtype=jnp.float32)
        return inp
    _L0_attn_in = _L0_attn_setup()

    def _L0_ffn_setup():
        import jax, jax.numpy as jnp
        import numpy as np
        E = 8
        K = 2
        CAP = 256
        H = 1024
        F = 4096
        key = jax.random.key(seed)
        ks = jax.random.split(key, 6)
        inp = {'hidden_states': jax.random.normal(ks[0], (2, 512, H), jnp.float32), 'router_w': jax.random.normal(ks[1], (E, H), jnp.float32) * (0.01 / np.sqrt(H)), 'w1': jax.random.normal(ks[2], (F, H), jnp.float32) * (1.0 / np.sqrt(H)), 'b1': jax.random.normal(ks[3], (F,), jnp.float32) * 0.01, 'w2': jax.random.normal(ks[4], (H, F), jnp.float32) * (1.0 / np.sqrt(F)), 'b2': jax.random.normal(ks[5], (H,), jnp.float32) * 0.01}
        return inp
    _L0_ffn_in = _L0_ffn_setup()
    _d = {'L0_attn_x': _L0_attn_in['x'], 'L0_attn_Wq': _L0_attn_in['Wq'], 'L0_attn_bq': _L0_attn_in['bq'], 'L0_attn_Wk': _L0_attn_in['Wk'], 'L0_attn_bk': _L0_attn_in['bk'], 'L0_attn_Wv': _L0_attn_in['Wv'], 'L0_attn_bv': _L0_attn_in['bv'], 'L0_attn_Wo': _L0_attn_in['Wo'], 'L0_attn_bo': _L0_attn_in['bo'], 'L0_ffn_router_w': _L0_ffn_in['router_w'], 'L0_ffn_w1': _L0_ffn_in['w1'], 'L0_ffn_b1': _L0_ffn_in['b1'], 'L0_ffn_w2': _L0_ffn_in['w2'], 'L0_ffn_b2': _L0_ffn_in['b2']}
    _x0 = _d['L0_attn_x']
    _d['L0_attn_x'] = jax.random.normal(jax.random.fold_in(jax.random.key(seed), 1), (4, 1024, 1024), dtype=_x0.dtype)
    del _x0
    return _d

def reference(L0_attn_x, L0_attn_Wq, L0_attn_bq, L0_attn_Wk, L0_attn_bk, L0_attn_Wv, L0_attn_bv, L0_attn_Wo, L0_attn_bo, L0_ffn_router_w, L0_ffn_w1, L0_ffn_b1, L0_ffn_w2, L0_ffn_b2):

    def _L0_attn_ref(x, Wq, bq, Wk, bk, Wv, bv, Wo, bo):
        import jax, jax.numpy as jnp
        import numpy as np
        D_MODEL = 1024
        N_HEADS = 16
        HEAD_DIM = D_MODEL // N_HEADS
        SCALE = HEAD_DIM ** (-0.5)
        B, L, D = x.shape
        H, Hd = (N_HEADS, HEAD_DIM)
        q = jnp.einsum('bld,ed->ble', x, Wq) + bq
        k = jnp.einsum('bld,ed->ble', x, Wk) + bk
        v = jnp.einsum('bld,ed->ble', x, Wv) + bv
        phi_q = jax.nn.elu(q) + 1.0
        phi_k = jax.nn.elu(k) + 1.0
        phi_q = phi_q.reshape(B, L, H, Hd)
        phi_k = phi_k.reshape(B, L, H, Hd)
        v = v.reshape(B, L, H, Hd)
        kv_sum = jnp.cumsum(phi_k * v, axis=1)
        context = (phi_q * kv_sum).reshape(B, L, D) * SCALE
        return jnp.einsum('bld,ed->ble', context, Wo) + bo

    def _L0_ffn_ref(hidden_states, router_w, w1, b1, w2, b2):
        import jax, jax.numpy as jnp
        import numpy as np
        E = 8
        K = 2
        CAP = 256
        H = 1024
        F = 4096
        orig_shape = hidden_states.shape
        x = hidden_states.reshape(-1, H)
        N = x.shape[0]
        logits = x @ router_w.T
        probs = jax.nn.softmax(logits, axis=-1)
        top_p, top_i = jax.lax.top_k(probs, K)
        expert_flat = top_i.T.reshape(-1)
        probs_flat = top_p.T.reshape(-1)
        token_idx = jnp.tile(jnp.arange(N), K)
        onehot = (expert_flat[:, None] == jnp.arange(E)[None, :]).astype(jnp.int32)
        pos = jnp.take_along_axis(jnp.cumsum(onehot, axis=0), expert_flat[:, None], axis=1)[:, 0] - 1
        keep = pos < CAP
        dest = expert_flat * CAP + pos
        dest_m = jnp.where(keep, dest, E * CAP)
        buf = jnp.zeros((E * CAP, H), x.dtype).at[dest_m].set(x[token_idx], mode='drop')
        h = jax.nn.gelu(buf @ w1.T + b1, approximate=False) @ w2.T + b2
        gathered = jnp.where(keep[:, None], h[jnp.where(keep, dest, 0)], 0.0) * probs_flat[:, None]
        out = jnp.zeros_like(x).at[token_idx].add(gathered)
        return out.reshape(orig_shape)
    x = L0_attn_x
    xn = _layernorm(x, axis=-1)
    s = _L0_attn_ref(xn, L0_attn_Wq, L0_attn_bq, L0_attn_Wk, L0_attn_bk, L0_attn_Wv, L0_attn_bv, L0_attn_Wo, L0_attn_bo)
    g = _silu(_L0_ffn_ref(xn, L0_ffn_router_w, L0_ffn_w1, L0_ffn_b1, L0_ffn_w2, L0_ffn_b2))
    x = x + s * g
    return x

_drawn_inputs = setup_inputs


def setup_inputs(seed=0):
    import zlib

    import numpy as np

    out = dict(_drawn_inputs(seed))
    spreads = {'L0_attn_bq': (0.0, 0.432),
     'L0_attn_bk': (0.0, 0.333),
     'L0_attn_bv': (0.0, 0.1),
     'L0_attn_bo': (0.0, 2.0)}
    factors = {'L0_ffn_b1': 8.0, 'L0_ffn_b2': 8.0}
    for name, (base, spread) in spreads.items():
        noise = np.random.default_rng([zlib.crc32(name.encode()), seed]).standard_normal(out[name].shape)
        drawn = base * np.exp(spread * noise) if base else spread * noise
        out[name] = jnp.asarray(drawn.astype(out[name].dtype))
    for name, factor in factors.items():
        out[name] = (out[name] * factor).astype(out[name].dtype)
    return out
```

```python
from contextlib import ExitStack

import numpy as np
import concourse.bass as bass
from concourse import mybir

F32 = mybir.dt.float32
F16 = mybir.dt.float16
I32 = mybir.dt.int32
U32 = mybir.dt.uint32
ALU = mybir.AluOpType
ACT = mybir.ActivationFunctionType
AX = mybir.AxisListType
ds = bass.ds

P = 128
TOKENS, D, F = 4096, 1024, 4096
SEQ = 1024
EXPERTS, TOPK, CAPACITY = 8, 2, 256
HEAD_DIM = 64
SCALE = HEAD_DIM ** -0.5
EPS = 1e-5

TILES = TOKENS // P
SEQ_TILES = SEQ // P
CH = D // P
SLOTS = EXPERTS * CAPACITY
SLOT_TILES = SLOTS // P
BLOCK = 512
BLOCKS = SLOTS // BLOCK
WIDE = SLOTS + P
GF = 256
FT = GF // P
ATT_GROUPS = D // GF
FFN_GROUPS = F // GF
GROUPS = ATT_GROUPS + FFN_GROUPS
PIECES = 4
NO_ROW = 8192

XS, WS, RS, KVS, CS, HS = 2.0 ** 5, 2.0 ** 8, 2.0 ** 12, 2.0 ** 4, 2.0 ** 2, 2.0 ** 4

HI, LO = 0, 1
PASSES = ((HI, HI), (HI, LO), (LO, HI))


class Chain:

    def __init__(self, eng, sem, base=0):
        self.eng, self.sem, self.base, self.n = eng, sem, base, 0

    def step(self, ins):
        ins.then_inc(self.sem, 1)
        self.n += 1

    def wait(self):
        self.eng.wait_ge(self.sem, self.base + self.n)

    def link(self, ins):
        self.step(ins)
        self.wait()


def apart(eng):
    eng.nop(nofuse=True)


def build(nc, x, w_kv, router, w_groups, b_k, b_v, b_q, b_o, b_1, b_2, out):
    kvs_dram = nc.dram_tensor("kvs_dram", (CH, P, WIDE), F32, kind="Internal").ap()
    s_dram = nc.dram_tensor("s_dram", (SLOT_TILES, P, D), F32, kind="Internal").ap()
    meta_dram = nc.dram_tensor("meta_dram", (SLOTS, 2), I32, kind="Internal").ap()

    x_tiles = x.rearrange("(t p) d -> t p d", p=P)
    win_dram = kvs_dram.rearrange("c p s -> p c s")

    with ExitStack() as ctx:
        def sb(name, shape, dt):
            return ctx.enter_context(nc.sbuf_tensor(name, shape, dt))

        def sem(name):
            return ctx.enter_context(nc.semaphore(name))

        arena_a = sb("arena_a", [P, SLOT_TILES * D], F32)
        wkv = arena_a[:, :].bitcast(F16).rearrange("p (q h e) -> p q h e", q=2 * CH, h=2)
        acc = arena_a[:, :].rearrange("p (t e) -> p t e", t=SLOT_TILES)
        xnT = sb("xnT", [P, 2, CH, WIDE], F16)
        AR = 14 * 1024
        arena_b = sb("arena_b", [P, AR], F32)

        def part(at, n):
            return arena_b[:, at * 1024:at * 1024 + n * 1024]

        x_in = [part(u, 1) for u in range(2)]
        x_hl = [part(2 + u, 1).bitcast(F16).rearrange("p (h d) -> p h d", h=2) for u in range(2)]
        xT = [part(4 + u, 1).bitcast(F16).rearrange("p (h c t) -> p h c t", h=2, c=CH) for u in range(2)]
        k_raw, k_exp, v_raw = part(6, 1), part(7, 1), part(8, 1)
        kv_hl = part(9, 1).bitcast(F16).rearrange("p (h e) -> p h e", h=2)
        window = [part(10 + u, 1).rearrange("p (c s) -> p c s", c=CH) for u in range(2)]
        bk_row, bv_row = part(12, 1), part(13, 1)

        ring = [part(4 * u, 4).bitcast(F16).rearrange("p (q h e) -> p q h e", q=PIECES, h=2)
                for u in range(2)]
        h_f32 = [arena_b[:, 8 * 1024 + BLOCK * f:8 * 1024 + BLOCK * (f + 1)] for f in range(FT)]
        h_hl = [part(9 + u, 1).bitcast(F16).rearrange("p (f h s) -> p f h s", f=FT, h=2) for u in range(2)]
        kvq = [arena_b[:, 11 * 1024 + BLOCK * f:11 * 1024 + BLOCK * (f + 1)] for f in range(FT)]
        q_exp = [arena_b[:, 12 * 1024 + BLOCK * f:12 * 1024 + BLOCK * (f + 1)] for f in range(FT)]
        def table(at, name_dims, **dims):
            n = int(np.prod(list(dims.values())))
            return arena_b[:, 6 * 1024 + at:6 * 1024 + at + n].rearrange(name_dims, **dims)

        N4 = TOPK * EXPERTS * TILES
        by_choice = dict(k=TOPK, e=EXPERTS, t=TILES)
        totals = table(0, "p (k e t) -> p k e t", **by_choice)
        running = table(N4, "p (k e t) -> p k e t", **by_choice)
        place = table(2 * N4, "p (k e t) -> p k e t", **by_choice)
        run_mask = table(3 * N4, "p (a t) -> p a t", a=TOPK * EXPERTS, t=TILES)
        logits = table(4 * N4, "p (t e) -> p t e", t=TILES, e=EXPERTS)
        top_v = table(4 * N4 + 256, "p (t e) -> p t e", t=TILES, e=EXPERTS)
        top_i = table(4 * N4 + 512, "p (t e) -> p t e", t=TILES, e=EXPERTS).bitcast(U32)
        chosen = arena_b[:, 6 * 1024 + 4 * N4 + 768:6 * 1024 + 4 * N4 + 1024].bitcast(F16)\
            .rearrange("p (k e t) -> p k e t", **by_choice)
        fx = [part(u, 1) for u in range(2)]
        fs = [part(2 + u, 1) for u in range(2)]
        fg = [part(4 + u, 1) for u in range(2)]

        stage = [sb(f"stage{u}", [P, 1024], F32) for u in range(2)]
        bias_row = sb("bias_row", [P, D], F32)

        ident = sb("ident", [P, P], F16)
        before = sb("before", [P, P], F16)
        ones = sb("ones", [P, P], F16)
        iota_i = sb("iota_i", [P, P], I32)
        iota = sb("iota", [P, P], F32)
        select = [sb(f"select{u}", [P, 2, P], F16) for u in range(2)]
        upto = [sb(f"upto{u}", [P, P], F16) for u in range(2)]
        rw_f = sb("rw_f", [P, CH, EXPERTS], F32)
        rw = sb("rw", [P, CH, 2, EXPERTS], F16)
        bq_c = sb("bq_c", [P, CH], F32)
        b1_c = sb("b1_c", [P, F // P], F32)
        eps_c = sb("eps_c", [P, 1], F32)

        bn = [sb(f"bn{u}", [P, 2, 6], F32) for u in range(2)]
        mv = [sb(f"mv{u}", [P, 2], F32) for u in range(2)]
        std = [sb(f"std{u}", [P, 1], F32) for u in range(2)]
        mean_t = sb("mean_t", [P, TILES + 2], F32)
        rstd_t = sb("rstd_t", [P, TILES + 2], F32)
        top_f = sb("top_f", [P, TOPK, TILES], F32)
        keep = sb("keep", [P, TOPK, TILES], F32)
        prob = sb("prob", [P, TOPK, TILES], F32)
        z = sb("z", [P, TILES], F32)
        small = sb("small", [P, 8, TILES], F32)
        kept_h = sb("kept_h", [P, TILES], F16)
        rank = sb("rank", [P, TILES + 2], F32)
        rank_kept = sb("rank_kept", [P, TILES + 2], F32)
        slot_i = sb("slot_i", [P, TILES], I32)
        start_i = sb("start_i", [P, TILES + 2], I32)
        loops_f = sb("loops_f", [P, 2], F32)
        loops_i = sb("loops_i", [P, 2], I32)
        meta = sb("meta", [P, TILES, 2], I32)
        meta_s = sb("meta_s", [P, SLOT_TILES, 2], I32)
        go_on = sb("go_on", [P, TILES + 2], F32)
        carry = sb("carry", [P, CH], F32)

        bank = [ctx.enter_context(nc.psum_tensor(f"pair{i}", [P, 2 * BLOCK], F32)) for i in range(4)]

        def out_bank(i):
            return bank[i // 2][:, (i % 2) * BLOCK:(i % 2 + 1) * BLOCK]

        const_ready = sem("const_ready")
        params_loaded = sem("params_loaded")
        rw_hi_ready, rw_ready = sem("rw_hi_ready"), sem("rw_ready")
        pool_chain = sem("pool_chain")
        filled = sem("filled")
        x_loaded = [sem(f"x_loaded{u}") for u in range(2)]
        var_ready, std_ready = sem("var_ready"), sem("std_ready")
        xn_ready, xhi_ready, xlo_ready = sem("xn_ready"), sem("xhi_ready"), sem("xlo_ready")
        thi_ready, tlo_ready = sem("thi_ready"), sem("tlo_ready")
        thi_read, tlo_read = sem("thi_read"), sem("tlo_read")
        logits_ready, logits_read = sem("logits_ready"), sem("logits_read")
        dve_router = sem("dve_router")
        wkv_loaded = [sem(f"wkv_loaded{u}") for u in range(2)]
        wkv_scaled, wkv_hi, wkv_ready = sem("wkv_scaled"), sem("wkv_hi"), sem("wkv_ready")
        dve_route = sem("dve_route")
        shifted, probs_ready = sem("shifted"), sem("probs_ready")
        chosen_ready, places_ready = sem("chosen_ready"), sem("places_ready")
        kept_ready, ranks_ready = sem("kept_ready"), sem("ranks_ready")
        tables_ready, meta_ready = sem("tables_ready"), sem("meta_ready")
        meta_filled, meta_stored, meta_loaded = sem("meta_filled"), sem("meta_stored"), sem("meta_loaded")
        rows_loaded = sem("rows_loaded")
        kx_loaded = [sem(f"kx_loaded{u}") for u in range(2)]
        kx_ready, kxhi_ready, kxlo_ready = sem("kx_ready"), sem("kxhi_ready"), sem("kxlo_ready")
        sel_ready = sem("sel_ready")
        stage_done, stage_dve, stage_act = sem("stage_done"), sem("stage_dve"), sem("stage_act")
        proj_done, proj_read = sem("proj_done"), sem("proj_read")
        kexp_ready, phik_ready = sem("kexp_ready"), sem("phik_ready")
        kv_ready, kvhi_ready, kvlo_ready = sem("kv_ready"), sem("kvhi_ready"), sem("kvlo_ready")
        win_ready, win_stored = sem("win_ready"), sem("win_stored")
        tail_stored = sem("tail_stored")
        sums_done, sums_stored = sem("sums_done"), sem("sums_stored")
        w_loaded = [sem(f"w_loaded{u}") for u in range(2)]
        whi_ready, wlo_ready = sem("whi_ready"), sem("wlo_ready")
        kvq_loaded = [sem(f"kvq_loaded{f}") for f in range(FT)]
        up_done, up_read = sem("up_done"), sem("up_read")
        hhi_ready, hlo_ready = sem("hhi_ready"), sem("hlo_ready")
        phi_ready, ctx_ready = sem("phi_ready"), sem("ctx_ready")
        down_done, down_added = sem("down_done"), sem("down_added")
        acc_ready, s_stored, b2_loaded = sem("acc_ready"), sem("s_stored"), sem("b2_loaded")
        copied = sem("copied")
        g_ready, fx_loaded, fs_loaded = sem("g_ready"), [sem(f"fx_loaded{u}") for u in range(2)], [sem(f"fs_loaded{u}") for u in range(2)]
        gated_ready, fin_ready, fin_stored = sem("gated_ready"), sem("fin_ready"), sem("fin_stored")

        block = ctx.enter_context(nc.Block())

        PARAM_LOADS = 3
        INV_XW = 1.0 / (XS * WS)
        STEPS = BLOCKS * GROUPS

        def read_selected(copy, u, s, pair, at, signal):
            c = slice(4 * (s % 2), 4 * (s % 2) + 4)
            both = bank[pair][:, :].rearrange("p (c w t) -> p c w t", c=4, w=2)
            copy(xT[u][:, s // 2, c, :], both[:, :, 0, :])
            copy(xnT[:, s // 2, c, at], both[:, :, 1, :]).then_inc(signal, 1)

        @block.sync
        def _(sp):
            sp.dma_start(rw_f[:, :, :], router).then_inc(params_loaded, 16)
            sp.dma_start(bq_c[:, :], b_q).then_inc(params_loaded, 16)
            sp.dma_start(b1_c[:, :], b_1).then_inc(params_loaded, 16)
            for row, src in ((bk_row, b_k), (bv_row, b_v), (bias_row[:, :], b_o)):
                sp.dma_start(row, src.to_broadcast((P, D))).then_inc(rows_loaded, 16)

            with sp.Fori(0, TILES // 2) as g:
                for u in range(2):
                    sp.wait_ge(xlo_ready, 2 * g + u + 1)
                    apart(sp)
                    sp.dma_start(x_in[u], x_tiles[2 * g + u]).then_inc(x_loaded[u], 16)

            sp.wait_ge(xlo_ready, 2 + TILES)
            for u in range(2):
                sp.dma_start(x_in[u], x_tiles[u]).then_inc(kx_loaded[u], 16)
            sp.wait_ge(tables_ready, 1)
            pairs = sp.value_load(loops_i[0:1, 0:1], min_val=1, max_val=TILES // 2)
            with sp.Fori(0, pairs) as g:
                for u in range(2):
                    t = 2 * g + u
                    sp.wait_ge(kxlo_ready, t + 1)
                    apart(sp)
                    sp.dma_start(x_in[u], x_tiles[(t + 2) % TILES]).then_inc(kx_loaded[u], 16)
                    at = sp.value_load(start_i[0:1, ds(t, 1)], min_val=0, max_val=SLOTS)
                    sp.wait_ge(win_ready, t + 2)
                    sp.wait_ge(win_stored, 16 * t + 32)
                    apart(sp)
                    sp.dma_start(win_dram[:, :, ds(at, P)], window[u]).then_inc(win_stored, 16)
            last = 2 * pairs
            at = sp.value_load(start_i[0:1, ds(last, 1)], min_val=0, max_val=SLOTS)
            sp.wait_ge(win_ready, last + 2)
            sp.wait_ge(win_stored, 16 * last + 32)
            apart(sp)
            sp.dma_start(win_dram[:, :, ds(at, P)], window[0]).then_inc(win_stored, 16)
            sp.wait_ge(win_stored, 16 * last + 48)
            apart(sp)
            kept = sp.value_load(start_i[0:1, TILES + 1:TILES + 2], min_val=0, max_val=SLOTS)
            tails = sp.value_load(loops_i[0:1, 1:2], min_val=1, max_val=SLOT_TILES + 1)
            with sp.Fori(0, tails) as n:
                at = nc.s_assert_within(kept + n * P, 0, SLOTS)
                sp.wait_ge(tail_stored, 16 * n + 16)
                apart(sp)
                sp.dma_start(win_dram[:, :, ds(at, P)], window[0]).then_inc(tail_stored, 16)
            sp.wait_ge(tail_stored, 16 * tails + 16)
            sp.nop().then_inc(sums_stored, 1)

            def piece(g, q):
                sp.dma_start(stage[q % 2][:, :], w_groups[g, :, q, :]).then_inc(w_loaded[q % 2], 16)

            sp.wait_ge(wkv_ready, 2 * CH)
            for q in range(PIECES):
                if q >= 2:
                    sp.wait_ge(wlo_ready, q - 1)
                piece(0, q)
            sp.wait_ge(sums_done, 1)

            def group_steps(grp, attention):
                for j in range(BLOCKS):
                    if attention:
                        for f in range(FT):
                            sp.wait_ge(ctx_ready, FT * (BLOCKS * grp + j - 1) + f + 1 + FT)
                            sp.dma_start(kvq[f], kvs_dram[FT * grp + f, :, j * BLOCK:(j + 1) * BLOCK])\
                              .then_inc(kvq_loaded[f], 16)
                    sp.wait_ge(wlo_ready, PIECES * grp + PIECES + j - 1)
                    piece((grp + 1) % GROUPS, j)

            with sp.Fori(0, ATT_GROUPS // 2) as g:
                for v in range(2):
                    group_steps(2 * g + v, True)
            with sp.Fori(0, FFN_GROUPS // 2) as g:
                for v in range(2):
                    group_steps(ATT_GROUPS + 2 * g + v, False)
            for u in range(2):
                sp.wait_ge(w_loaded[u], 16 * 2 * (GROUPS + 1))

            for st in range(SLOT_TILES):
                u = st % 2
                if st == 0:
                    sp.wait_ge(wlo_ready, PIECES * (GROUPS + 1))
                    sp.wait_ge(down_done, 16 + 8 * STEPS)
                if st >= 2:
                    sp.wait_ge(fin_ready, st - 1)
                sp.dma_start(fs[u], s_dram[st]).then_inc(fs_loaded[u], 16)
            sp.wait_ge(fs_loaded[0], 16 * (SLOT_TILES // 2))
            sp.wait_ge(fs_loaded[1], 16 * (SLOT_TILES // 2))

        @block.gpsimd
        def _(pool):
            ch = Chain(pool, pool_chain)
            nc.gpsimd.memset(ones[:, :], 1.0)
            nc.gpsimd.memset(eps_c[:, :], EPS)
            nc.gpsimd.memset(mean_t[:, TILES:TILES + 2], 0.0)
            nc.gpsimd.memset(rstd_t[:, TILES:TILES + 2], 0.0)
            nc.gpsimd.memset(rank[:, TILES:TILES + 2], 0.0)
            nc.gpsimd.memset(rank_kept[:, TILES:TILES + 2], -1.0)
            nc.gpsimd.memset(run_mask[:, :, :], 1.0)
            nc.gpsimd.memset(go_on[:, :], 1.0)
            nc.gpsimd.iota(iota_i[:, :], [[1, P]], base=0, channel_multiplier=0)
            nc.gpsimd.iota(meta[:, :, 0], [[P, TILES]], base=0, channel_multiplier=1)
            nc.gpsimd.memset(meta_s[:, :, 0], NO_ROW)
            nc.gpsimd.memset(meta_s[:, :, 1], 0)
            ch.link(nc.gpsimd.memset(ident[:, :], 0.0))
            for t in range(0, TILES + 2, SEQ_TILES):
                nc.gpsimd.memset(go_on[:, t:t + 1], 0.0)
            nc.gpsimd.memset(run_mask[:, :, 0:1], 0.0)
            nc.gpsimd.affine_select(out=before[:, :], in_=ones[:, :], pattern=[[1, P]], compare_op=ALU.is_gt,
                                    fill=0.0, base=0, channel_multiplier=-1)
            ch.link(nc.gpsimd.affine_select(out=ident[:, :], in_=ident[:, :], pattern=[[-1, P]],
                                            compare_op=ALU.not_equal, fill=1.0, base=0,
                                            channel_multiplier=1))
            for u in range(2):
                last = nc.gpsimd.tensor_copy(select[u][:, 0, :], ident[:, :])
            last.then_inc(const_ready, 1)
            pool.dma_start(meta_dram.rearrange("(t p) c -> p t c", p=P), meta_s[:, :, :]).then_inc(meta_filled, 16)
            nc.gpsimd.memset(xnT[:, :, :, :].rearrange("p h c s -> p (h c s)").bitcast(F32), 0.0).then_inc(filled, 1)

            with pool.Fori(0, CH) as g:
                for u in range(2):
                    pool.dma_start(stage[u][:, :], w_kv[2 * g + u]).then_inc(wkv_loaded[u], 16)
                for u in range(2):
                    q = 2 * g + u
                    pool.wait_ge(wkv_loaded[u], 16 * g + 16)
                    apart(pool)
                    nc.gpsimd.tensor_scalar(stage[u][:, :], stage[u][:, :], WS, None, ALU.mult)\
                      .then_inc(wkv_scaled, 1)
                    pool.wait_ge(wkv_scaled, q + 1)
                    hi = wkv[:, ds(q, 1), HI, :].rearrange("p a e -> p (a e)")
                    lo = wkv[:, ds(q, 1), LO, :].rearrange("p a e -> p (a e)")
                    nc.gpsimd.tensor_copy(hi, stage[u][:, :]).then_inc(wkv_hi, 1)
                    pool.wait_ge(wkv_hi, q + 1)
                    nc.gpsimd.tensor_tensor(lo, stage[u][:, :], hi, ALU.subtract).then_inc(wkv_ready, 1)
                pool.wait_ge(wkv_ready, 2 * g + 2)

            pool.wait_ge(meta_ready, 1)
            pool.wait_ge(meta_filled, 16)
            for t in range(TILES):
                pool.indirect_dma_start(
                    meta_dram, bass.IndirectOffsetOnAxis(ap=slot_i[:, t:t + 1].bitcast(U32), axis=0), meta[:, t, :], None,
                    bounds_check=SLOTS - 1, oob_is_err=False).then_inc(meta_stored, 16)
            pool.wait_ge(meta_stored, 16 * TILES)
            pool.dma_start(meta_s[:, :, :], meta_dram.rearrange("(t p) c -> p t c", p=P)).then_inc(meta_loaded, 16)

            pool.wait_ge(sums_done, 1)
            pool.wait_ge(rows_loaded, 48)
            for b in range(SLOT_TILES):
                ins = nc.gpsimd.tensor_copy(acc[:, b, :], bias_row[:, :])
                if b % BLOCKS == BLOCKS - 1:
                    ins.then_inc(acc_ready, 1)
            for n in range(8):
                rows = TOKENS // 8
                pool.dma_start(out[n * rows:(n + 1) * rows, :].rearrange("(a r) d -> a (r d)", a=16),
                               x[n * rows:(n + 1) * rows, :].rearrange("(a r) d -> a (r d)", a=16))\
                    .then_inc(copied, 16)
            pool.wait_ge(acc_ready, BLOCKS)
            pool.dma_start(bias_row[:, :], b_2.to_broadcast((P, D))).then_inc(b2_loaded, 16)
            pool.wait_ge(b2_loaded, 16)
            ATT_STEPS = ATT_GROUPS * BLOCKS
            for b in range(BLOCKS):
                pool.wait_ge(down_added, 4 + 8 * (ATT_STEPS - BLOCKS + b + 1))
                rows = slice(b * (BLOCK // P), (b + 1) * (BLOCK // P))
                pool.dma_start(s_dram[rows].rearrange("t p e -> p t e"), acc[:, rows, :]).then_inc(s_stored, 16)
                pool.wait_ge(s_stored, 16 * (b + 1))
                for st in range(b * (BLOCK // P), (b + 1) * (BLOCK // P)):
                    ins = nc.gpsimd.tensor_copy(acc[:, st, :], bias_row[:, :])
                ins.then_inc(acc_ready, 1)

            pool.wait_ge(meta_loaded, 16)
            pool.wait_ge(copied, 16 * 8)
            pool.wait_ge(wlo_ready, PIECES * (GROUPS + 1))
            pool.wait_ge(down_done, 16 + 8 * STEPS)

            def row_of(st):
                return bass.IndirectOffsetOnAxis(ap=meta_s[:, st, 0:1].bitcast(U32), axis=0)

            def finish(st):
                pool.wait_ge(fin_ready, st + 1)
                pool.indirect_dma_start(out, row_of(st), fx[st % 2], None,
                                        bounds_check=TOKENS - 1, oob_is_err=False).then_inc(fin_stored, 16)

            for st in range(SLOT_TILES):
                if st >= 2:
                    pool.wait_ge(fin_stored, 16 * (st - 1))
                pool.indirect_dma_start(fx[st % 2], None, x, row_of(st), bounds_check=TOKENS - 1,
                                        oob_is_err=False).then_inc(fx_loaded[st % 2], 16)
                if st >= 1:
                    finish(st - 1)
            finish(SLOT_TILES - 1)
            pool.wait_ge(fin_stored, 16 * SLOT_TILES)

        @block.scalar
        def _(act):
            act.wait_ge(params_loaded, 16 * PARAM_LOADS)
            nc.scalar.activation(rw[:, :, HI, :], rw_f[:, :, :], ACT.Copy, scale=RS).then_inc(rw_hi_ready, 1)
            act.wait_ge(const_ready, 1)

            with act.Fori(0, TILES // 2) as g:
                for u in range(2):
                    t = 2 * g + u
                    act.wait_ge(var_ready, t + 1)
                    nc.scalar.activation(std[u][:, :], mv[u][:, 1:2], ACT.Sqrt, bias=eps_c[:, 0:1]).then_inc(std_ready, 1)
                for u in range(2):
                    act.wait_ge(xn_ready, 2 * g + u + 1)
                    nc.scalar.activation(x_hl[u][:, HI, :], x_in[u], ACT.Copy, scale=XS).then_inc(xhi_ready, 1)
                for u in range(2):
                    t = 2 * g + u
                    act.wait_ge(thi_ready, t + 1)
                    act.wait_ge(logits_read, t + 1)
                    nc.scalar.activation(xT[u][:, HI].rearrange("p c t -> p (c t)"), bank[0][:, :], ACT.Copy)\
                      .then_inc(thi_read, 1)

            act.wait_ge(shifted, 1)
            nc.scalar.activation(logits[:, :, :], logits[:, :, :], ACT.Exp)
            nc.scalar.activation(prob[:, :, :], prob[:, :, :], ACT.Exp).then_inc(probs_ready, 1)

            def split_x(u, n):
                act.wait_ge(kx_ready, n)
                nc.scalar.activation(x_hl[u][:, HI, :], x_in[u], ACT.Copy, scale=XS).then_inc(kxhi_ready, 1)

            split_x(0, 1)
            split_x(1, 2)
            def copy(dst, src):
                return nc.scalar.activation(dst, src, ACT.Copy)

            act.wait_ge(filled, 1)
            for s in (0, 2):
                act.wait_ge(stage_done, s + 1)
                read_selected(copy, 0, s, 2, slice(0, P), stage_act)
            act.wait_ge(tables_ready, 1)
            pairs = act.value_load(loops_i[0:1, 0:1], min_val=1, max_val=TILES // 2)
            with act.Fori(0, pairs) as g:
                for u in range(2):
                    t = 2 * g + u

                    def exp_k(half):
                        act.wait_ge(proj_read, 4 + 4 * t + half + 1)
                        act.wait_ge(kv_ready, 2 * t + half + 1)
                        e = slice(half * BLOCK, (half + 1) * BLOCK)
                        nc.scalar.activation(k_exp[:, e], k_raw[:, e], ACT.Exp)
                        nc.scalar.activation(k_raw[:, e], k_raw[:, e], ACT.Relu).then_inc(kexp_ready, 1)

                    exp_k(0)
                    at = act.value_load(start_i[0:1, ds(t + 2, 1)], min_val=0, max_val=SLOTS)
                    for s in (0, 2):
                        act.wait_ge(stage_done, 5 * t + 4 + 1 + s + 1)
                        apart(act)
                        read_selected(copy, 1 - u, s, 2 + (u + 1 + s) % 2, ds(at, P), stage_act)
                    exp_k(1)
                    act.wait_ge(kx_ready, t + 3)
                    nc.scalar.activation(x_hl[u][:, HI, :], x_in[u], ACT.Copy, scale=XS).then_inc(kxhi_ready, 1)
                    for half in range(2):
                        act.wait_ge(kv_ready, 2 + 2 * t + half + 1)
                        e = slice(half * BLOCK, (half + 1) * BLOCK)
                        nc.scalar.activation(kv_hl[:, HI, e], v_raw[:, e], ACT.Copy, scale=KVS).then_inc(kvhi_ready, 1)

            def piece_hi(grp, par, q):
                act.wait_ge(w_loaded[q % 2], 16 * (2 * grp + q // 2 + 1))
                nc.scalar.activation(ring[par][:, q, HI, :], stage[q % 2][:, :], ACT.Copy, scale=WS)\
                  .then_inc(whi_ready, 1)

            act.wait_ge(sums_done, 1)
            for q in range(PIECES):
                piece_hi(0, 0, q)
            act.wait_ge(sums_stored, 1)

            def group_steps(grp, par, attention):
                for j in range(BLOCKS):
                    s = BLOCKS * grp + j
                    for f in range(FT):
                        act.wait_ge(up_done, FT * s + f + 1)
                        act.wait_ge(hlo_ready, FT * s + f + 1)
                        apart(act)
                        src = out_bank(FT * (j % 2) + f)
                        if attention:
                            bias = bq_c[:, ds(FT * grp + f, 1)]
                            nc.scalar.activation(q_exp[f], src, ACT.Exp, bias=bias, scale=INV_XW)
                            nc.scalar.activation(h_f32[f], src, ACT.Relu, bias=bias, scale=INV_XW).then_inc(up_read, 1)
                        else:
                            bias = b1_c[:, ds(FT * (grp - ATT_GROUPS) + f, 1)]
                            nc.scalar.activation(h_f32[f], src, ACT.Gelu, bias=bias, scale=INV_XW).then_inc(up_read, 1)
                    for f in range(FT):
                        if attention:
                            act.wait_ge(ctx_ready, FT * s + f + 1 + FT)
                        else:
                            act.wait_ge(up_read, 4 + FT * s + f + 1)
                        act.wait_ge(down_done, 8 * s + 8)
                        nc.scalar.activation(h_hl[j % 2][:, f, HI, :], h_f32[f], ACT.Copy,
                                             scale=1.0 if attention else HS).then_inc(hhi_ready, 1)
                    if j >= 2:
                        act.wait_ge(down_done, 8 * s)
                    piece_hi(grp + 1, 1 - par, j)

            with act.Fori(0, ATT_GROUPS // 2) as g:
                for v in range(2):
                    group_steps(2 * g + v, v, True)
            with act.Fori(0, FFN_GROUPS // 2) as g:
                for v in range(2):
                    group_steps(ATT_GROUPS + 2 * g + v, v, False)

            act.wait_ge(meta_loaded, 16)
            for st in range(SLOT_TILES):
                act.wait_ge(down_added, 4 + 8 * (BLOCKS * GROUPS - BLOCKS + st // BLOCKS + 1))
                if st == 0:
                    act.wait_ge(down_done, 16 + 8 * STEPS)
                if st >= 2:
                    act.wait_ge(fin_ready, st - 1)
                nc.scalar.activation(fg[st % 2], acc[:, st, :], ACT.Silu,
                                     scale=meta_s[:, st, 1:2].bitcast(F32)).then_inc(g_ready, 1)

        @block.vector
        def _(dve):
            scratch = [small[:, 0, n:n + 1] for n in range(TILES)]
            for i, (s, n) in enumerate(((xlo_ready, 2), (logits_read, 2), (proj_read, 4), (win_stored, 32), (tail_stored, 16),
                         (kv_ready, 2), (up_read, 4), (down_done, 16), (down_added, 4), (hlo_ready, FT),
                         (ctx_ready, FT))):
                nc.vector.memset(scratch[i], 0.0).then_inc(s, n)
            dve.wait_ge(rw_hi_ready, 1)
            nc.vector.scalar_tensor_tensor(rw[:, :, LO, :], rw_f[:, :, :], RS, rw[:, :, HI, :],
                                           ALU.mult, ALU.subtract).then_inc(rw_ready, 1)
            dve.wait_ge(const_ready, 1)
            nc.vector.tensor_copy(iota[:, :], iota_i[:, :])

            with dve.Fori(0, TILES // 2) as g:
                own = Chain(dve, dve_router, base=6 * g)
                for u in range(2):
                    dve.wait_ge(x_loaded[u], 16 * g + 16)
                    for half in range(2):
                        ins = nc.vector.bn_stats(bn[u][:, half, :], x_in[u][:, half * 512:(half + 1) * 512])
                    own.link(ins)
                    apart(dve)
                    nc.vector.bn_aggr(mv[u][:, :], bn[u][:, :, :].rearrange("p a b -> p (a b)")).then_inc(var_ready, 1)
                for u in range(2):
                    t = 2 * g + u
                    dve.wait_ge(std_ready, t + 1)
                    own.step(nc.vector.tensor_copy(mean_t[:, ds(t, 1)], mv[u][:, 0:1]))
                    own.link(nc.vector.reciprocal(rstd_t[:, ds(t, 1)], std[u][:, :]))
                    nc.vector.tensor_scalar(x_in[u], x_in[u], mean_t[:, ds(t, 1)], rstd_t[:, ds(t, 1)],
                                            ALU.subtract, ALU.mult).then_inc(xn_ready, 1)
                assert own.n == 6
                for u in range(2):
                    t = 2 * g + u
                    dve.wait_ge(xhi_ready, t + 1)
                    nc.vector.scalar_tensor_tensor(x_hl[u][:, LO, :], x_in[u], XS, x_hl[u][:, HI, :],
                                                   ALU.mult, ALU.subtract).then_inc(xlo_ready, 1)
                for u in range(2):
                    t = 2 * g + u
                    dve.wait_ge(tlo_ready, t + 1)
                    nc.vector.tensor_copy(xT[u][:, LO].rearrange("p c t -> p (c t)"), bank[1][:, :]).then_inc(tlo_read, 1)
                for u in range(2):
                    t = 2 * g + u
                    dve.wait_ge(logits_ready, t + 1)
                    nc.vector.tensor_reduce(logits[:, ds(t, 1), :].rearrange("p a e -> p (a e)"),
                                            bank[2 + u][:, 0:2 * EXPERTS].rearrange("p (h e) -> p e h", h=2),
                                            AX.X, ALU.add).then_inc(logits_read, 1)

            own = Chain(dve, dve_route)
            dve.wait_ge(logits_read, 2 + TILES)
            flat = logits[:, :, :].rearrange("p t e -> p (t e)")
            own.link(nc.vector.tensor_scalar(flat, flat, 1.0 / (XS * RS), None, ALU.mult))
            for t in range(TILES):
                ins = nc.vector.max(top_v[:, t, :], logits[:, t, :])
            own.link(ins)
            for t in range(TILES):
                ins = nc.vector.max_index(top_i[:, t, :], top_v[:, t, :], logits[:, t, :])
            own.link(ins)
            for k in range(TOPK):
                nc.vector.tensor_tensor(prob[:, k, :], top_v[:, :, k], top_v[:, :, 0], ALU.subtract)
            for t in range(TILES):
                ins = nc.vector.tensor_scalar(logits[:, t, :], logits[:, t, :], top_v[:, t, 0:1], None, ALU.subtract)
            ins.then_inc(shifted, 1)
            for k in range(TOPK):
                ins = nc.vector.tensor_copy(top_f[:, k, :], top_i[:, :, k])
            own.link(ins)
            for k in range(TOPK):
                for e in range(EXPERTS):
                    ins = nc.vector.tensor_scalar(chosen[:, k, e, :], top_f[:, k, :], float(e), None, ALU.is_equal)
            ins.then_inc(chosen_ready, 1)

            def flat4(a):
                return a[:, :, :, :].rearrange("p k e t -> p (k e t)")

            dve.wait_ge(places_ready, 1)
            own.link(nc.vector.tensor_copy(flat4(totals), out_bank(1)))
            own.link(nc.vector.tensor_tensor_scan(flat4(running), run_mask[:, :, :].rearrange("p a t -> p (a t)"),
                                                  flat4(totals), 0.0, ALU.mult, ALU.add))
            own.link(nc.vector.tensor_tensor(flat4(place), flat4(running), flat4(totals), ALU.subtract))
            own.link(nc.vector.tensor_tensor(flat4(place), flat4(place), out_bank(0), ALU.add))
            for e in range(EXPERTS):
                ins = nc.vector.tensor_scalar(place[:, 1, e, :], place[:, 1, e, :], running[:, 0, e, TILES - 1:TILES],
                                              None, ALU.add)
            own.link(ins)
            own.link(nc.vector.scalar_tensor_tensor(flat4(place), flat4(place), float(CAPACITY), flat4(chosen),
                                                    ALU.is_lt, ALU.mult))
            own.link(nc.vector.tensor_reduce(keep[:, :, :], place[:, :, :, :].rearrange("p k e t -> p k t e"),
                                             AX.X, ALU.add))
            kept = small[:, 1, :]
            own.link(nc.vector.tensor_tensor(kept, keep[:, 0, :], keep[:, 1, :], ALU.max))
            nc.vector.tensor_copy(kept_h[:, :], kept).then_inc(kept_ready, 1)
            dve.wait_ge(probs_ready, 1)
            own.link(nc.vector.tensor_reduce(z[:, :], logits[:, :, :], AX.X, ALU.add))
            own.link(nc.vector.reciprocal(z[:, :], z[:, :]))
            own.link(nc.vector.tensor_tensor(prob[:, :, :], prob[:, :, :], keep[:, :, :], ALU.mult))
            own.link(nc.vector.tensor_tensor(prob[:, 0, :], prob[:, 0, :], prob[:, 1, :], ALU.add))
            own.link(nc.vector.tensor_tensor(meta[:, :, 1].bitcast(F32), prob[:, 0, :], z[:, :], ALU.mult))
            dve.wait_ge(ranks_ready, 1)
            tile_kept, run_kept, start = small[:, 2, :], small[:, 3, :], small[:, 4, :]
            nc.vector.tensor_copy(rank[:, 0:TILES], bank[0][:, 0:TILES])
            own.link(nc.vector.tensor_copy(tile_kept, bank[1][:, 0:TILES]))
            own.link(nc.vector.tensor_tensor_scan(run_kept, run_mask[:, 0, :], tile_kept, 0.0, ALU.mult, ALU.add))
            own.link(nc.vector.tensor_tensor(start, run_kept, tile_kept, ALU.subtract))
            nc.vector.memset(start_i[:, 0:1], 0)
            nc.vector.tensor_copy(start_i[:, 1:TILES + 1], start)
            nc.vector.tensor_copy(start_i[:, TILES + 1:TILES + 2], run_kept[:, TILES - 1:TILES])
            own.link(nc.vector.tensor_tensor(start, start, rank[:, 0:TILES], ALU.add))
            own.link(nc.vector.scalar_tensor_tensor(start, start, -float(NO_ROW), kept, ALU.add, ALU.mult))
            own.link(nc.vector.tensor_scalar(start, start, float(NO_ROW), None, ALU.add))
            nc.vector.tensor_copy(slot_i[:, :], start).then_inc(meta_ready, 1)
            own.link(nc.vector.scalar_tensor_tensor(rank_kept[:, 0:TILES], rank[:, 0:TILES], 1.0, kept,
                                                    ALU.add, ALU.mult))
            own.link(nc.vector.tensor_scalar(rank_kept[:, 0:TILES], rank_kept[:, 0:TILES], -1.0, None, ALU.add))
            last_tile, count = small[:, 5, :], small[:, 6, :]
            own.link(nc.vector.scalar_tensor_tensor(last_tile, tile_kept, 0.0, iota[:, 1:TILES + 1],
                                                    ALU.is_gt, ALU.mult))
            own.link(nc.vector.tensor_reduce(loops_f[:, 0:1], last_tile, AX.X, ALU.max))
            own.link(nc.vector.tensor_scalar(count[:, 0:TILES // 2], iota[:, 0:TILES // 2], 2.0, loops_f[:, 0:1],
                                             ALU.mult, ALU.is_lt))
            own.link(nc.vector.tensor_reduce(loops_f[:, 0:1], count[:, 0:TILES // 2], AX.X, ALU.add))
            tail_starts = iota[:, 0:SLOT_TILES + 1]
            own.link(nc.vector.tensor_scalar(loops_f[:, 1:2], run_kept[:, TILES - 1:TILES], -1.0, float(SLOTS),
                                             ALU.mult, ALU.add))
            own.link(nc.vector.tensor_scalar(count[:, 0:SLOT_TILES + 1], tail_starts, float(P), loops_f[:, 1:2],
                                             ALU.mult, ALU.is_le))
            own.link(nc.vector.tensor_reduce(loops_f[:, 1:2], count[:, 0:SLOT_TILES + 1], AX.X, ALU.add))
            own.link(nc.vector.tensor_copy(loops_i[:, :], loops_f[:, :]))

            nc.vector.memset(carry[:, :], 0.0).then_inc(win_ready, 1)
            nc.vector.memset(upto[1][:, :], 0.0)
            nc.vector.memset(kv_hl[:, :, :], 0.0).then_inc(kvlo_ready, 2)
            nc.vector.memset(scratch[30], 0.0).then_inc(tables_ready, 1)
            dve.wait_ge(tables_ready, 1)

            def norm_x(u, col, loaded):
                dve.wait_ge(kx_loaded[u], loaded)
                nc.vector.tensor_scalar(x_in[u], x_in[u], mean_t[:, ds(col, 1)], rstd_t[:, ds(col, 1)],
                                        ALU.subtract, ALU.mult).then_inc(kx_ready, 1)
                nc.vector.tensor_scalar(select[u][:, 1, :], iota[:, :], rank_kept[:, ds(col, 1)], None, ALU.is_equal)

            def low_x(u, n):
                dve.wait_ge(kxhi_ready, n)
                nc.vector.scalar_tensor_tensor(x_hl[u][:, LO, :], x_in[u], XS, x_hl[u][:, HI, :],
                                               ALU.mult, ALU.subtract).then_inc(kxlo_ready, 1)

            norm_x(0, 0, 16)
            norm_x(1, 1, 16)
            low_x(0, 1)
            low_x(1, 2)
            dve.wait_ge(filled, 1)
            for s in (1, 3):
                dve.wait_ge(stage_done, s + 1)
                read_selected(nc.vector.tensor_copy, 0, s, 3, slice(0, P), stage_dve)
            dve.wait_ge(rows_loaded, 48)
            pairs = dve.value_load(loops_i[0:1, 0:1], min_val=1, max_val=TILES // 2)

            def sums(u, t, n):
                dve.wait_ge(stage_done, n + 1)
                dve.wait_ge(win_stored, 16 * t + 16)
                dve.wait_ge(win_ready, t + 1)
                w = window[u]
                for c in range(2):
                    ins = nc.vector.scalar_tensor_tensor(
                        w[:, 4 * c:4 * c + 4, :],
                        bank[2 + u][:, c * BLOCK:(c + 1) * BLOCK].rearrange("p (c s) -> p c s", c=4), 1.0 / KVS,
                        carry[:, 4 * c:4 * c + 4].unsqueeze(2).to_broadcast((P, 4, P)), ALU.mult, ALU.add)
                ins.then_inc(stage_dve, 1)
                dve.wait_ge(stage_dve, 3 * t + 3)
                nc.vector.tensor_scalar(carry[:, :], w[:, :, P - 1], go_on[:, ds(t, 1)], None, ALU.mult)\
                  .then_inc(win_ready, 1)

            with dve.Fori(0, pairs) as g:
                for u in range(2):
                    t = 2 * g + u
                    e = [slice(h * BLOCK, (h + 1) * BLOCK) for h in range(2)]

                    def read_k(half):
                        dve.wait_ge(proj_done, 4 * t + half + 1)
                        nc.vector.scalar_tensor_tensor(k_raw[:, e[half]], out_bank(half), INV_XW, bk_row[:, e[half]],
                                                       ALU.mult, ALU.add).then_inc(proj_read, 1)

                    read_k(0)
                    sums(u, t, 5 * t + 4)
                    at = dve.value_load(start_i[0:1, ds(t + 2, 1)], min_val=0, max_val=SLOTS)
                    for s in (1, 3):
                        dve.wait_ge(stage_done, 5 * t + 4 + 1 + s + 1)
                        read_selected(nc.vector.tensor_copy, 1 - u, s, 2 + (u + 1 + s) % 2, ds(at, P), stage_dve)
                    read_k(1)
                    norm_x(u, t + 2, 16 * g + 32)
                    nc.vector.tensor_scalar(upto[u][:, :], iota[:, :], rank[:, ds(t, 1)], None, ALU.is_ge)
                    for half in range(2):
                        dve.wait_ge(kexp_ready, 2 * t + half + 1)
                        ins = nc.vector.scalar_tensor_tensor(k_exp[:, e[half]], k_exp[:, e[half]], 1.0,
                                                             k_raw[:, e[half]], ALU.min, ALU.add)
                        ins.then_inc(phik_ready, 1)
                    low_x(u, t + 3)
                    for half in range(2):
                        dve.wait_ge(proj_done, 4 * t + 2 + half + 1)
                        own_v = nc.vector.scalar_tensor_tensor(v_raw[:, e[half]], out_bank(2 + half), INV_XW,
                                                               bv_row[:, e[half]], ALU.mult, ALU.add)
                        own_v.then_inc(proj_read, 1)
                        dve.wait_ge(proj_read, 4 + 4 * t + 2 + half + 1)
                        dve.wait_ge(phik_ready, 2 * t + half + 1)
                        nc.vector.tensor_tensor(v_raw[:, e[half]], v_raw[:, e[half]], k_exp[:, e[half]], ALU.mult)\
                          .then_inc(kv_ready, 1)
                    for half in range(2):
                        dve.wait_ge(kvhi_ready, 2 * t + half + 1)
                        ins = nc.vector.scalar_tensor_tensor(kv_hl[:, LO, e[half]], v_raw[:, e[half]], KVS,
                                                             kv_hl[:, HI, e[half]], ALU.mult, ALU.subtract)
                        ins.then_inc(kvlo_ready, 1)
            last = 2 * pairs
            sums(0, last, 10 * pairs + 4)
            nc.vector.memset(scratch[31], 0.0).then_inc(sums_done, 1)

            def piece_lo(grp, par, q):
                dve.wait_ge(whi_ready, PIECES * grp + q + 1)
                nc.vector.scalar_tensor_tensor(ring[par][:, q, LO, :], stage[q % 2][:, :], WS, ring[par][:, q, HI, :],
                                               ALU.mult, ALU.subtract).then_inc(wlo_ready, 1)

            for q in range(PIECES):
                piece_lo(0, 0, q)

            def low_h(s, j, attention):
                for f in range(FT):
                    dve.wait_ge(hhi_ready, FT * s + f + 1)
                    nc.vector.scalar_tensor_tensor(h_hl[j % 2][:, f, LO, :], h_f32[f], 1.0 if attention else HS,
                                                   h_hl[j % 2][:, f, HI, :], ALU.mult, ALU.subtract).then_inc(hlo_ready, 1)

            def add_down(s, j, factor, start_count):
                dve.wait_ge(acc_ready, start_count)
                for m in range(8):
                    dve.wait_ge(down_done, 16 + 8 * s + m + 1)
                    row = acc[:, 4 * (j % BLOCKS) + m // 2, (m % 2) * BLOCK:(m % 2 + 1) * BLOCK]
                    nc.vector.scalar_tensor_tensor(row, out_bank(4 + m % 4), factor, row, ALU.mult, ALU.add)\
                      .then_inc(down_added, 1)

            def contexts(s, grp, j):
                for f in range(FT):
                    dve.wait_ge(up_read, 4 + FT * s + f + 1)
                    nc.vector.scalar_tensor_tensor(h_f32[f], q_exp[f], 1.0, h_f32[f], ALU.min, ALU.add).then_inc(phi_ready, 1)
                for f in range(FT):
                    dve.wait_ge(phi_ready, FT * s + f + 1)
                    dve.wait_ge(kvq_loaded[f], 16 * s + 16)
                    nc.vector.scalar_tensor_tensor(h_f32[f], h_f32[f], SCALE * CS, kvq[f], ALU.mult, ALU.mult)\
                      .then_inc(ctx_ready, 1)

            def body(base_group, attention, factor, count_at):
                n = 2 * BLOCKS
                for j in range(n + 1):
                    if j < n:
                        s = BLOCKS * base_group + j
                        grp = base_group + j // BLOCKS
                        if attention:
                            contexts(s, grp, j)
                        low_h(s, j, attention)
                        piece_lo(grp + 1, 1 - j // BLOCKS, j % BLOCKS)
                    if j >= 1:
                        add_down(BLOCKS * base_group + j - 1, j - 1, factor, count_at((j - 1) % BLOCKS))

            with dve.Fori(0, ATT_GROUPS // 2) as g:
                body(2 * g, True, 1.0 / (CS * WS), lambda b: b + 1)
            with dve.Fori(0, FFN_GROUPS // 2) as g:
                body(ATT_GROUPS + 2 * g, False, 1.0 / (HS * WS), lambda b: BLOCKS + b + 1)

            for st in range(SLOT_TILES):
                u = st % 2
                dve.wait_ge(g_ready, st + 1)
                dve.wait_ge(fs_loaded[u], 16 * (st // 2 + 1))
                nc.vector.tensor_tensor(fs[u], fs[u], fg[u], ALU.mult).then_inc(gated_ready, 1)
                dve.wait_ge(gated_ready, st + 1)
                dve.wait_ge(fx_loaded[u], 16 * (st // 2 + 1))
                nc.vector.tensor_tensor(fx[u], fx[u], fs[u], ALU.add).then_inc(fin_ready, 1)

        @block.tensor
        def _(pe):
            mm = nc.tensor.matmul
            pe.wait_ge(const_ready, 1)
            pe.wait_ge(rw_ready, 1)

            with pe.Fori(0, TILES // 2) as g:
                for u in range(2):
                    t = 2 * g + u
                    for h, have, n, done, pair in ((HI, xhi_ready, t + 1, thi_ready, 0),
                                                   (LO, xlo_ready, t + 3, tlo_ready, 1)):
                        pe.wait_ge(have, n)
                        for c in range(CH):
                            ins = mm(bank[pair][:, c * P:(c + 1) * P], x_hl[u][:, h, c * P:(c + 1) * P], ident[:, :],
                                     start=True, stop=True)
                        ins.then_inc(done, 1)
                    pe.wait_ge(thi_read, t + 1)
                    pe.wait_ge(tlo_read, t + 1)
                    pe.wait_ge(logits_read, t + 1)
                    for n, (h, c) in enumerate((h, c) for h in (HI, LO) for c in range(CH)):
                        ins = mm(bank[2 + u][:, 0:2 * EXPERTS], xT[u][:, h, c, :],
                                 rw[:, c, :, :].rearrange("p h e -> p (h e)"), start=(n == 0), stop=(n == 2 * CH - 1))
                    ins.then_inc(logits_ready, 1)

            pe.wait_ge(chosen_ready, 1)
            picks = chosen[:, :, :, :].rearrange("p k e t -> p (k e t)")
            mm(out_bank(0), before[:, :], picks, start=True, stop=True)
            mm(out_bank(1), ones[:, :], picks, start=True, stop=True).then_inc(places_ready, 1)
            pe.wait_ge(kept_ready, 1)
            mm(bank[0][:, 0:TILES], before[:, :], kept_h[:, :], start=True, stop=True)
            mm(bank[1][:, 0:TILES], ones[:, :], kept_h[:, :], start=True, stop=True).then_inc(ranks_ready, 1)

            def select_x(u, s, pair):
                for c in range(4):
                    cc = 4 * (s % 2) + c
                    ins = mm(bank[pair][:, c * 2 * P:(c + 1) * 2 * P], x_hl[u][:, s // 2, cc * P:(cc + 1) * P],
                             select[u][:, :, :].rearrange("p w t -> p (w t)"), start=True, stop=True)
                ins.then_inc(stage_done, 1)

            pe.wait_ge(tables_ready, 1)
            pe.wait_ge(kxlo_ready, 1)
            for s in range(4):
                if s >= 2:
                    pe.wait_ge((stage_act, stage_dve)[s % 2], 1)
                select_x(0, s, 2 + s % 2)
            pe.wait_ge(wkv_ready, 2 * CH)
            pairs = pe.value_load(loops_i[0:1, 0:1], min_val=1, max_val=TILES // 2)

            def project(u, t, n):
                pe.wait_ge(proj_read, 4 * t + n + 1)
                e = slice((n % 2) * BLOCK, (n % 2 + 1) * BLOCK)
                k = 0
                for c in range(CH):
                    for a, b in PASSES:
                        ins = mm(out_bank(n), xT[u][:, a, c, :], wkv[:, (n // 2) * CH + c, b, e],
                                 start=(k == 0), stop=(k == 3 * CH - 1))
                        k += 1
                ins.then_inc(proj_done, 1)

            def sum_kv(u, par, n):
                for c in range(CH):
                    for h in (HI, LO):
                        ins = mm(bank[2 + u][:, c * P:(c + 1) * P], kv_hl[:, h, c * P:(c + 1) * P], upto[par][:, :],
                                 start=(h == HI), stop=(h == LO))
                ins.then_inc(stage_done, 1)

            with pe.Fori(0, pairs) as g:
                for u in range(2):
                    t = 2 * g + u
                    pe.wait_ge(stage_act, 2 * t + 2)
                    pe.wait_ge(stage_dve, 3 * t + 2)
                    project(u, t, 0)
                    pe.wait_ge(kvlo_ready, 2 * t + 2)
                    sum_kv(u, 1 - u, 5 * t + 4)
                    pe.wait_ge(kxlo_ready, t + 2)
                    for s in range(4):
                        if s == 2:
                            project(u, t, 1)
                        if s == 1 or s == 3:
                            pe.wait_ge(stage_dve, 3 * t + (3 if s == 1 else 4))
                        if s == 2:
                            pe.wait_ge(stage_act, 2 * t + 3)
                        select_x(1 - u, s, 2 + (u + 1 + s) % 2)
                    project(u, t, 2)
                    project(u, t, 3)
            pe.wait_ge(kvlo_ready, 4 * pairs + 2)
            pe.wait_ge(stage_dve, 6 * pairs + 2)
            pe.wait_ge(stage_act, 4 * pairs + 2)
            sum_kv(0, 1, 10 * pairs + 4)

            def up(s, j, grp, par):
                pe.wait_ge(wlo_ready, PIECES * grp + 2)
                for f in range(FT):
                    pe.wait_ge(up_read, FT * s + f + 1)
                    k = 0
                    for c in range(CH):
                        w = ring[par][:, c // 4, :, :].rearrange("p h (c n) -> p h c n", c=4)
                        for a, b in PASSES:
                            ins = mm(out_bank(FT * (j % 2) + f), w[:, a, c % 4, f * P:(f + 1) * P],
                                     xnT[:, b, c, (j % BLOCKS) * BLOCK:(j % BLOCKS + 1) * BLOCK],
                                     start=(k == 0), stop=(k == 3 * CH - 1))
                            k += 1
                    ins.then_inc(up_done, 1)

            def down(s, j, grp, par):
                pe.wait_ge(wlo_ready, PIECES * grp + PIECES)
                pe.wait_ge(hlo_ready, FT * s + FT + FT)
                for m in range(8):
                    pe.wait_ge(down_added, 8 * s + m + 1)
                    k = 0
                    for f in range(FT):
                        for a, b in PASSES:
                            ins = mm(out_bank(4 + m % 4), h_hl[j % 2][:, f, a, (m // 2) * P:(m // 2 + 1) * P],
                                     ring[par][:, 2 + f, b, (m % 2) * BLOCK:(m % 2 + 1) * BLOCK],
                                     start=(k == 0), stop=(k == 3 * FT - 1))
                            k += 1
                    ins.then_inc(down_done, 1)

            def body(base_group):
                n = 2 * BLOCKS
                for j in range(n + 1):
                    if j < n:
                        up(BLOCKS * base_group + j, j, base_group + j // BLOCKS, j // BLOCKS)
                    if j >= 1:
                        down(BLOCKS * base_group + j - 1, j - 1, base_group + (j - 1) // BLOCKS, (j - 1) // BLOCKS)

            with pe.Fori(0, GROUPS // 2) as g:
                body(2 * g)


_OUTS = [((4, 1024, 1024), "float32")]


def kernel(L0_attn_x, L0_attn_Wq, L0_attn_bq, L0_attn_Wk, L0_attn_bk, L0_attn_Wv, L0_attn_bv, L0_attn_Wo,
           L0_attn_bo, L0_ffn_router_w, L0_ffn_w1, L0_ffn_b1, L0_ffn_w2, L0_ffn_b2):
    import concourse.bacc as bacc
    from concourse.bass_utils import run_bass_kernel_spmd

    def rows_in(w):
        return np.asarray(w).T.reshape(-1, P, w.shape[0])

    def groups(up, down, n):
        a = rows_in(up).reshape(CH, P, n, GF).transpose(2, 1, 0, 3).reshape(n, P, 2, 1024)
        b = rows_in(down).reshape(n, FT, P, D).transpose(0, 2, 1, 3)
        return np.concatenate([a, b], axis=2)

    def columns(b):
        return np.asarray(b).reshape(-1, P).T

    arrays = {
        "x": np.asarray(L0_attn_x).reshape(TOKENS, D),
        "w_kv": np.concatenate([rows_in(L0_attn_Wk), rows_in(L0_attn_Wv)]),
        "router": rows_in(L0_ffn_router_w).transpose(1, 0, 2),
        "w_groups": np.concatenate([groups(L0_attn_Wq, L0_attn_Wo, ATT_GROUPS),
                                    groups(L0_ffn_w1, L0_ffn_w2, FFN_GROUPS)]),
        "b_k": np.asarray(L0_attn_bk).reshape(1, D), "b_v": np.asarray(L0_attn_bv).reshape(1, D),
        "b_q": columns(L0_attn_bq), "b_o": np.asarray(L0_attn_bo).reshape(1, D),
        "b_1": columns(L0_ffn_b1), "b_2": np.asarray(L0_ffn_b2).reshape(1, D),
    }
    arrays = {n: np.ascontiguousarray(a) for n, a in arrays.items()}
    nc = bacc.Bacc("TRN2", target_bir_lowering=False, num_devices=1)
    args = [nc.dram_tensor(n, a.shape, F32, kind="ExternalInput").ap() for n, a in arrays.items()]
    out = nc.dram_tensor("out", (TOKENS, D), F32, kind="ExternalOutput").ap()
    build(nc, *args, out)
    r = run_bass_kernel_spmd(nc, [arrays], core_ids=[0])
    return r.results[0]["out"].reshape(4, 1024, 1024)
```

```python
from contextlib import ExitStack

import numpy as np
import concourse.bass as bass
from concourse import mybir

F32 = mybir.dt.float32
F16 = mybir.dt.float16
I32 = mybir.dt.int32
U32 = mybir.dt.uint32
ALU = mybir.AluOpType
ACT = mybir.ActivationFunctionType
AX = mybir.AxisListType
ds = bass.ds

P = 128
TOKENS, D, F = 4096, 1024, 4096
SEQ = 1024
EXPERTS, TOPK, CAPACITY = 8, 2, 256
HEAD_DIM = 64
SCALE = HEAD_DIM ** -0.5
EPS = 1e-5

TILES = TOKENS // P
TOKEN_BLOCKS = TOKENS // 512
SEQ_TILES = SEQ // P
CH = D // P
SLOTS = EXPERTS * CAPACITY
SLOT_TILES = SLOTS // P
BLOCK = 512
BLOCKS = SLOTS // BLOCK
WIDE = SLOTS + P
GF = 256
FT = GF // P
ATT_GROUPS = D // GF
FFN_GROUPS = F // GF
GROUPS = ATT_GROUPS + FFN_GROUPS
PIECES = 4
NO_ROW = 8192

XS, WS, RS, KVS, CS, HS = 2.0 ** 5, 2.0 ** 8, 2.0 ** 12, 2.0 ** 4, 2.0 ** 2, 2.0 ** 4

HI, LO = 0, 1
PASSES = ((HI, HI), (HI, LO), (LO, HI))


class Chain:

    def __init__(self, eng, sem, base=0):
        self.eng, self.sem, self.base, self.n = eng, sem, base, 0

    def step(self, ins):
        ins.then_inc(self.sem, 1)
        self.n += 1

    def wait(self):
        self.eng.wait_ge(self.sem, self.base + self.n)

    def link(self, ins):
        self.step(ins)
        self.wait()


def apart(eng):
    eng.nop(nofuse=True)


def build(nc, x, x_t, w_kv, router, w_groups, b_k, b_v, b_q, b_o, b_1, b_2, out):
    kvs_dram = nc.dram_tensor("kvs_dram", (CH, P, WIDE), F32, kind="Internal").ap()
    s_dram = nc.dram_tensor("s_dram", (SLOT_TILES, P, D), F32, kind="Internal").ap()
    meta_dram = nc.dram_tensor("meta_dram", (SLOTS, 2), I32, kind="Internal").ap()

    x_tiles = x.rearrange("(t p) d -> t p d", p=P)
    win_dram = kvs_dram.rearrange("c p s -> p c s")

    with ExitStack() as ctx:
        def sb(name, shape, dt):
            return ctx.enter_context(nc.sbuf_tensor(name, shape, dt))

        def sem(name):
            return ctx.enter_context(nc.semaphore(name))

        arena_a = sb("arena_a", [P, SLOT_TILES * D], F32)
        wkv = arena_a[:, :].bitcast(F16).rearrange("p (q h e) -> p q h e", q=2 * CH, h=2)
        acc = arena_a[:, :].rearrange("p (t e) -> p t e", t=SLOT_TILES)
        xnT = sb("xnT", [P, 2, CH, WIDE], F16)
        AR = 14 * 1024
        arena_b = sb("arena_b", [P, AR], F32)

        def part(at, n):
            return arena_b[:, at * 1024:at * 1024 + n * 1024]

        x_in = [part(u, 1) for u in range(2)]
        x_hl = [part(2 + u, 1).bitcast(F16).rearrange("p (h d) -> p h d", h=2) for u in range(2)]
        xT = [part(4 + u, 1).bitcast(F16).rearrange("p (h c t) -> p h c t", h=2, c=CH) for u in range(2)]
        k_raw, k_exp, v_raw = part(6, 1), part(7, 1), part(8, 1)
        kv_hl = part(9, 1).bitcast(F16).rearrange("p (h e) -> p h e", h=2)
        window = [part(10 + u, 1).rearrange("p (c s) -> p c s", c=CH) for u in range(2)]
        bk_row, bv_row = part(12, 1), part(13, 1)

        ring = [part(4 * u, 4).bitcast(F16).rearrange("p (q h e) -> p q h e", q=PIECES, h=2)
                for u in range(2)]
        h_f32 = [arena_b[:, 8 * 1024 + BLOCK * f:8 * 1024 + BLOCK * (f + 1)] for f in range(FT)]
        h_hl = [part(9 + u, 1).bitcast(F16).rearrange("p (f h s) -> p f h s", f=FT, h=2) for u in range(2)]
        kvq = [arena_b[:, 11 * 1024 + BLOCK * f:11 * 1024 + BLOCK * (f + 1)] for f in range(FT)]
        q_exp = [arena_b[:, 12 * 1024 + BLOCK * f:12 * 1024 + BLOCK * (f + 1)] for f in range(FT)]
        xnT_f = xnT[:, :, :, :].rearrange("p h c s -> p (h c s)").bitcast(F32)
        k_stage = [xnT_f[:, 1024 * c:1024 * (c + 1)] for c in range(CH)]

        def table(at, name_dims, **dims):
            n = int(np.prod(list(dims.values())))
            at += 1024 * CH
            return xnT_f[:, at:at + n].rearrange(name_dims, **dims)

        N4 = TOPK * EXPERTS * TILES
        by_choice = dict(k=TOPK, e=EXPERTS, t=TILES)
        totals = table(0, "p (k e t) -> p k e t", **by_choice)
        running = table(N4, "p (k e t) -> p k e t", **by_choice)
        place = table(2 * N4, "p (k e t) -> p k e t", **by_choice)
        run_mask = table(3 * N4, "p (a t) -> p a t", a=TOPK * EXPERTS, t=TILES)
        top_v = table(4 * N4, "p (t e) -> p t e", t=TILES, e=EXPERTS)
        top_i = table(4 * N4 + 256, "p (t e) -> p t e", t=TILES, e=EXPERTS).bitcast(U32)
        chosen = xnT_f[:, 1024 * CH + 4 * N4 + 512:1024 * CH + 4 * N4 + 768].bitcast(F16)\
            .rearrange("p (k e t) -> p k e t", **by_choice)
        sums_x = table(4 * N4 + 768, "p (t e) -> p t e", t=TILES, e=EXPERTS + 1)
        iota_i = xnT_f[:, 1024 * CH + 4 * N4 + 1100:1024 * CH + 4 * N4 + 1100 + P].bitcast(I32)
        ones_f = xnT_f[:, 1024 * CH + 4 * N4 + 1300:1024 * CH + 4 * N4 + 1300 + P]
        top_f = table(4 * N4 + 1500, "p (k t) -> p k t", k=TOPK, t=TILES)
        by_expert = [xnT_f[:, 12288 + BLOCK * u:12288 + BLOCK * (u + 1)] for u in range(2)]
        ident_f = xnT_f[:, 13312:13312 + EXPERTS + 1]
        xt_in = [part(2 + 4 * u, 4).rearrange("p (c t) -> p c t", c=CH) for u in range(2)]
        FX = 4
        fx = [part(i, 1) for i in range(FX)]
        fs = [part(11 + u, 1) for u in range(2)]

        stage = [sb(f"stage{u}", [P, 1024], F32) for u in range(2)]
        bias_row = sb("bias_row", [P, D], F32)
        fg = [part(13, 1), bias_row[:, :]]
        v_stage = [part(9, 1), part(6, 1), part(7, 1), part(8, 1), part(10, 1), part(11, 1),
                   stage[0][:, :], stage[1][:, :]]

        ident = sb("ident", [P, P], F16)
        before = sb("before", [P, P], F16)
        ones = sb("ones", [P, P], F16)
        iota = sb("iota", [P, P], F32)
        select = [sb(f"select{u}", [P, 2, P], F16) for u in range(2)]
        upto = [sb(f"upto{u}", [P, P], F16) for u in range(2)]
        rw_f = sb("rw_f", [P, CH, EXPERTS + 1], F32)
        rw_sum = sb("rw_sum", [P, EXPERTS], F32)
        logits = sb("logits", [P, TILES, EXPERTS], F32)
        bq_c = sb("bq_c", [P, CH], F32)
        b1_c = sb("b1_c", [P, F // P], F32)
        eps_c = sb("eps_c", [P, 1], F32)
        power_c = sb("power_c", [P, 1], F32)
        zero_c = sb("zero_c", [P, 1], F16)

        bn = [sb(f"bn{u}", [P, 2, 6], F32) for u in range(2)]
        mv = [sb(f"mv{u}", [P, 2], F32) for u in range(2)]
        var = [sb(f"var{u}", [P, 1], F32) for u in range(2)]
        rstd = [sb(f"rstd{u}", [P, 1], F32) for u in range(2)]
        rstd_t = sb("rstd_t", [P, TILES + 2], F32)
        keep = sb("keep", [P, TOPK, TILES], F32)
        prob = sb("prob", [P, TOPK, TILES], F32)
        z = sb("z", [P, TILES], F32)
        small = sb("small", [P, 8, TILES], F32)
        kept_h = sb("kept_h", [P, TILES], F16)
        rank = sb("rank", [P, TILES + 2], F32)
        rank_kept = sb("rank_kept", [P, TILES + 2], F32)
        slot_i = sb("slot_i", [P, TILES], I32)
        start_i = sb("start_i", [P, TILES + 2], I32)
        loops_f = sb("loops_f", [P, 2], F32)
        loops_i = sb("loops_i", [P, 2], I32)
        meta = sb("meta", [P, TILES, 2], I32)
        meta_s = sb("meta_s", [P, SLOT_TILES, 2], I32)
        go_on = sb("go_on", [P, TILES + 2], F32)
        carry = sb("carry", [P, CH], F32)

        bank = [ctx.enter_context(nc.psum_tensor(f"pair{i}", [P, 2 * BLOCK], F32)) for i in range(4)]

        def out_bank(i):
            return bank[i // 2][:, (i % 2) * BLOCK:(i % 2 + 1) * BLOCK]

        const_ready, ident_ready = sem("const_ready"), sem("ident_ready")
        params_loaded = sem("params_loaded")
        pool_chain = sem("pool_chain")
        xt_loaded = [sem(f"xt_loaded{u}") for u in range(2)]
        scores_done, scores_read, logits_done = sem("scores_done"), sem("scores_read"), sem("logits_done")
        wkv_loaded = [sem(f"wkv_loaded{q}") for q in range(2 * CH)]
        wkv_hi, wkv_ready = sem("wkv_hi"), sem("wkv_ready")
        dve_route, dve_weights = sem("dve_route"), sem("dve_weights")
        scaled, probs_ready = sem("scaled"), sem("probs_ready")
        chosen_ready, places_ready = sem("chosen_ready"), sem("places_ready")
        kept_ready, ranks_ready = sem("kept_ready"), sem("ranks_ready")
        tables_ready, meta_ready = sem("tables_ready"), sem("meta_ready")
        meta_filled, meta_stored, meta_loaded = sem("meta_filled"), sem("meta_stored"), sem("meta_loaded")
        rows_loaded = sem("rows_loaded")
        kx_loaded = [sem(f"kx_loaded{u}") for u in range(2)]
        stats_ready, var_ready, var_eps, rstd_ready = (sem(n) for n in ("stats_ready", "var_ready", "var_eps", "rstd_ready"))
        kx_ready, kxhi_ready, kxlo_ready = sem("kx_ready"), sem("kxhi_ready"), sem("kxlo_ready")
        stage_done, stage_dve, stage_act = sem("stage_done"), sem("stage_dve"), sem("stage_act")
        proj_done, proj_read = sem("proj_done"), sem("proj_read")
        kexp_ready, phik_ready = sem("kexp_ready"), sem("phik_ready")
        kv_ready, kvhi_ready, kvlo_ready = sem("kv_ready"), sem("kvhi_ready"), sem("kvlo_ready")
        win_ready, win_stored = sem("win_ready"), sem("win_stored")
        tail_stored = sem("tail_stored")
        sums_done, sums_stored = sem("sums_done"), sem("sums_stored")
        w_loaded = [sem(f"w_loaded{u}") for u in range(2)]
        whi_ready, wlo_ready = sem("whi_ready"), sem("wlo_ready")
        kvq_loaded = [sem(f"kvq_loaded{f}") for f in range(FT)]
        up_done, up_read = sem("up_done"), sem("up_read")
        hhi_ready, hlo_ready = sem("hhi_ready"), sem("hlo_ready")
        phi_ready, ctx_ready = sem("phi_ready"), sem("ctx_ready")
        down_done, down_added = sem("down_done"), sem("down_added")
        acc_ready, s_stored, b2_loaded = sem("acc_ready"), sem("s_stored"), sem("b2_loaded")
        copied = sem("copied")
        g_ready, fx_loaded, fs_loaded = sem("g_ready"), [sem(f"fx_loaded{i}") for i in range(FX)], [sem(f"fs_loaded{u}") for u in range(2)]
        gated_ready, fin_ready, fin_stored = sem("gated_ready"), sem("fin_ready"), sem("fin_stored")

        block = ctx.enter_context(nc.Block())

        PARAM_LOADS = 3
        INV_XW = 1.0 / (XS * WS)
        STEPS = BLOCKS * GROUPS

        def scores(u):
            return bank[2][0:EXPERTS + 1, u * BLOCK:(u + 1) * BLOCK]

        def read_selected(copy, u, s, pair, at, signal):
            c = slice(4 * (s % 2), 4 * (s % 2) + 4)
            both = bank[pair][:, :].rearrange("p (c w t) -> p c w t", c=4, w=2)
            copy(xT[u][:, s // 2, c, :], both[:, :, 0, :])
            copy(xnT[:, s // 2, c, at], both[:, :, 1, :]).then_inc(signal, 1)

        @block.sync
        def _(sp):
            sp.dma_start(rw_f[:, :, 0:EXPERTS], router).then_inc(params_loaded, 16)
            sp.dma_start(bq_c[:, :], b_q).then_inc(params_loaded, 16)
            sp.dma_start(b1_c[:, :], b_1).then_inc(params_loaded, 16)
            for row, src in ((bk_row, b_k), (bv_row, b_v), (bias_row[:, :], b_o)):
                sp.dma_start(row, src.to_broadcast((P, D))).then_inc(rows_loaded, 16)

            for u in range(2):
                sp.dma_start(x_in[u], x_tiles[u]).then_inc(kx_loaded[u], 16)
            for b in range(TOKEN_BLOCKS):
                if b >= 2:
                    sp.wait_ge(scores_done, b - 1)
                sp.dma_start(xt_in[b % 2], x_t[b]).then_inc(xt_loaded[b % 2], 16)
                sp.dma_start(k_stage[b], w_kv[b]).then_inc(wkv_loaded[b], 16)
            sp.wait_ge(scores_done, TOKEN_BLOCKS)
            for q in range(CH, 2 * CH):
                sp.dma_start(v_stage[q - CH], w_kv[q]).then_inc(wkv_loaded[q], 16)

            def piece(g, q):
                sp.dma_start(stage[q % 2][:, :], w_groups[g, :, q, :]).then_inc(w_loaded[q % 2], 16)

            sp.wait_ge(wkv_ready, 2 * CH)
            for q in range(2):
                piece(0, q)

            sp.wait_ge(tables_ready, 1)
            pairs = sp.value_load(loops_i[0:1, 0:1], min_val=1, max_val=TILES // 2)
            with sp.Fori(0, pairs) as g:
                for u in range(2):
                    t = 2 * g + u
                    sp.wait_ge(kxlo_ready, t + 1)
                    apart(sp)
                    sp.dma_start(x_in[u], x_tiles[(t + 2) % TILES]).then_inc(kx_loaded[u], 16)
                    at = sp.value_load(start_i[0:1, ds(t, 1)], min_val=0, max_val=SLOTS)
                    sp.wait_ge(win_ready, t + 2)
                    sp.wait_ge(win_stored, 16 * t + 32)
                    apart(sp)
                    sp.dma_start(win_dram[:, :, ds(at, P)], window[u]).then_inc(win_stored, 16)
            last = 2 * pairs
            at = sp.value_load(start_i[0:1, ds(last, 1)], min_val=0, max_val=SLOTS)
            sp.wait_ge(win_ready, last + 2)
            sp.wait_ge(win_stored, 16 * last + 32)
            apart(sp)
            sp.dma_start(win_dram[:, :, ds(at, P)], window[0]).then_inc(win_stored, 16)
            sp.wait_ge(win_stored, 16 * last + 48)
            apart(sp)
            kept = sp.value_load(start_i[0:1, TILES + 1:TILES + 2], min_val=0, max_val=SLOTS)
            tails = sp.value_load(loops_i[0:1, 1:2], min_val=1, max_val=SLOT_TILES + 1)
            with sp.Fori(0, tails) as n:
                at = nc.s_assert_within(kept + n * P, 0, SLOTS)
                sp.wait_ge(tail_stored, 16 * n + 16)
                apart(sp)
                sp.dma_start(win_dram[:, :, ds(at, P)], window[0]).then_inc(tail_stored, 16)
            sp.wait_ge(tail_stored, 16 * tails + 16)
            sp.nop().then_inc(sums_stored, 1)

            for q in range(2, PIECES):
                sp.wait_ge(wlo_ready, q - 1)
                piece(0, q)
            sp.wait_ge(sums_done, 1)

            def copy_rows(n):
                rows = TOKENS // FFN_GROUPS
                sp.dma_start(out.rearrange("(n a r) d -> n a (r d)", n=FFN_GROUPS, a=16)[n],
                             x.rearrange("(n a r) d -> n a (r d)", n=FFN_GROUPS, a=16)[n]).then_inc(copied, 16)

            def group_steps(grp, attention):
                for j in range(BLOCKS):
                    if attention:
                        for f in range(FT):
                            sp.wait_ge(ctx_ready, FT * (BLOCKS * grp + j - 1) + f + 1 + FT)
                            sp.dma_start(kvq[f], kvs_dram[FT * grp + f, :, j * BLOCK:(j + 1) * BLOCK])\
                              .then_inc(kvq_loaded[f], 16)
                    sp.wait_ge(wlo_ready, PIECES * grp + PIECES + j - 1)
                    piece(grp + 1, j)

            with sp.Fori(0, ATT_GROUPS // 2) as g:
                for v in range(2):
                    group_steps(2 * g + v, True)
            with sp.Fori(0, FFN_GROUPS // 2 - 1) as g:
                for v in range(2):
                    copy_rows(2 * g + v)
                    group_steps(ATT_GROUPS + 2 * g + v, False)
            copy_rows(FFN_GROUPS - 2)
            copy_rows(FFN_GROUPS - 1)
            group_steps(GROUPS - 2, False)

            sp.wait_ge(down_done, 16 + 8 * (STEPS - BLOCKS))
            for st in range(SLOT_TILES):
                u = st % 2
                if st >= 2:
                    sp.wait_ge(fin_ready, st - 1)
                sp.dma_start(fs[u], s_dram[st]).then_inc(fs_loaded[u], 16)
            sp.wait_ge(fs_loaded[0], 16 * (SLOT_TILES // 2))
            sp.wait_ge(fs_loaded[1], 16 * (SLOT_TILES // 2))

        @block.gpsimd
        def _(pool):
            ch = Chain(pool, pool_chain)
            nc.gpsimd.memset(ones[:, :], 1.0)
            nc.gpsimd.memset(ones_f, 1.0)
            nc.gpsimd.memset(rw_f[:, :, EXPERTS:EXPERTS + 1], 1.0)
            nc.gpsimd.memset(eps_c[:, :], EPS)
            nc.gpsimd.memset(power_c[:, :], -0.5)
            nc.gpsimd.memset(zero_c[:, :], 0.0)
            nc.gpsimd.memset(rstd_t[:, :], 0.0)
            nc.gpsimd.memset(rank[:, TILES:TILES + 2], 0.0)
            nc.gpsimd.memset(rank_kept[:, TILES:TILES + 2], -1.0)
            nc.gpsimd.memset(run_mask[:, :, :], 1.0)
            nc.gpsimd.memset(go_on[:, :], 1.0)
            nc.gpsimd.iota(iota_i, [[1, P]], base=0, channel_multiplier=0)
            nc.gpsimd.iota(meta[:, :, 0], [[P, TILES]], base=0, channel_multiplier=1)
            nc.gpsimd.memset(meta_s[:, :, 0], NO_ROW)
            nc.gpsimd.memset(meta_s[:, :, 1], 0)
            ch.link(nc.gpsimd.memset(ident[:, :], 0.0))
            for t in range(0, TILES + 2, SEQ_TILES):
                nc.gpsimd.memset(go_on[:, t:t + 1], 0.0)
            nc.gpsimd.memset(run_mask[:, :, 0:1], 0.0)
            nc.gpsimd.affine_select(out=before[:, :], in_=ones[:, :], pattern=[[1, P]], compare_op=ALU.is_gt,
                                    fill=0.0, base=0, channel_multiplier=-1)
            ch.link(nc.gpsimd.affine_select(out=ident[:, :], in_=ident[:, :], pattern=[[-1, P]],
                                            compare_op=ALU.not_equal, fill=1.0, base=0,
                                            channel_multiplier=1))
            for u in range(2):
                last = nc.gpsimd.tensor_copy(select[u][:, 0, :], ident[:, :])
            last.then_inc(const_ready, 1)
            pool.dma_start(meta_dram.rearrange("(t p) c -> p t c", p=P), meta_s[:, :, :]).then_inc(meta_filled, 16)

            def reciprocal_deviation(u, n):
                pool.wait_ge(var_ready, n)
                nc.gpsimd.tensor_tensor(var[u][:, :], mv[u][:, 1:2], eps_c[:, :], ALU.add).then_inc(var_eps, 1)
                pool.wait_ge(var_eps, n)
                nc.gpsimd.tensor_tensor(rstd[u][:, :], var[u][:, :], power_c[:, :], ALU.pow).then_inc(rstd_ready, 1)

            reciprocal_deviation(0, 1)
            reciprocal_deviation(1, 2)
            pool.wait_ge(tables_ready, 1)
            pairs = pool.value_load(loops_i[0:1, 0:1], min_val=1, max_val=TILES // 2)
            with pool.Fori(0, pairs) as g:
                for u in range(2):
                    reciprocal_deviation(u, 2 * g + u + 3)

            pool.wait_ge(sums_done, 1)
            pool.wait_ge(rows_loaded, 48)
            for b in range(SLOT_TILES):
                ins = nc.gpsimd.tensor_copy(acc[:, b, :], bias_row[:, :])
                if b % BLOCKS == BLOCKS - 1:
                    ins.then_inc(acc_ready, 1)
            pool.wait_ge(meta_ready, 1)
            pool.wait_ge(meta_filled, 16)
            for t in range(TILES):
                pool.indirect_dma_start(
                    meta_dram, bass.IndirectOffsetOnAxis(ap=slot_i[:, t:t + 1].bitcast(U32), axis=0), meta[:, t, :], None,
                    bounds_check=SLOTS - 1, oob_is_err=False).then_inc(meta_stored, 16)
            pool.wait_ge(meta_stored, 16 * TILES)
            pool.dma_start(meta_s[:, :, :], meta_dram.rearrange("(t p) c -> p t c", p=P)).then_inc(meta_loaded, 16)

            pool.wait_ge(acc_ready, BLOCKS)
            pool.dma_start(bias_row[:, :], b_2.to_broadcast((P, D))).then_inc(b2_loaded, 16)
            pool.wait_ge(b2_loaded, 16)
            ATT_STEPS = ATT_GROUPS * BLOCKS
            for b in range(BLOCKS):
                pool.wait_ge(down_added, 4 + 8 * (ATT_STEPS - BLOCKS + b + 1))
                rows = slice(b * (BLOCK // P), (b + 1) * (BLOCK // P))
                pool.dma_start(s_dram[rows].rearrange("t p e -> p t e"), acc[:, rows, :]).then_inc(s_stored, 16)
                pool.wait_ge(s_stored, 16 * (b + 1))
                for st in range(b * (BLOCK // P), (b + 1) * (BLOCK // P)):
                    ins = nc.gpsimd.tensor_copy(acc[:, st, :], bias_row[:, :])
                ins.then_inc(acc_ready, 1)

            pool.wait_ge(meta_loaded, 16)
            pool.wait_ge(down_done, 16 + 8 * (STEPS - BLOCKS))
            pool.wait_ge(copied, 16 * FFN_GROUPS)

            def row_of(st):
                return bass.IndirectOffsetOnAxis(ap=meta_s[:, st, 0:1].bitcast(U32), axis=0)

            for st in range(SLOT_TILES + FX - 1):
                if st < SLOT_TILES:
                    if st >= FX:
                        pool.wait_ge(fin_stored, 16 * (st - FX + 1))
                    pool.indirect_dma_start(fx[st % FX], None, x, row_of(st), bounds_check=TOKENS - 1,
                                            oob_is_err=False).then_inc(fx_loaded[st % FX], 16)
                done = st - (FX - 1)
                if done >= 0:
                    pool.wait_ge(fin_ready, done + 1)
                    pool.indirect_dma_start(out, row_of(done), fx[done % FX], None,
                                            bounds_check=TOKENS - 1, oob_is_err=False).then_inc(fin_stored, 16)
            pool.wait_ge(fin_stored, 16 * SLOT_TILES)

        @block.scalar
        def _(act):
            act.wait_ge(params_loaded, 16 * PARAM_LOADS)
            act.wait_ge(const_ready, 1)

            def high_wkv(q):
                act.wait_ge(wkv_loaded[q], 16)
                nc.scalar.activation(wkv[:, q, HI, :], (k_stage + v_stage)[q], ACT.Copy, scale=WS).then_inc(wkv_hi, 1)

            for b in range(TOKEN_BLOCKS):
                act.wait_ge(scores_done, b + 1)
                if b >= 2:
                    act.wait_ge(logits_done, b - 1)
                nc.scalar.activation(by_expert[b % 2][0:EXPERTS + 1, :], scores(b % 2), ACT.Copy).then_inc(scores_read, 1)
                high_wkv(b)
            for u in range(2):
                act.wait_ge(kx_ready, u + 1)
                nc.scalar.activation(x_hl[u][:, HI, :], x_in[u], ACT.Copy, scale=XS).then_inc(kxhi_ready, 1)
            for q in range(CH, 2 * CH):
                high_wkv(q)

            def copy(dst, src):
                return nc.scalar.activation(dst, src, ACT.Copy)

            for s in (0, 2):
                act.wait_ge(stage_done, s + 1)
                read_selected(copy, 0, s, 2, slice(0, P), stage_act)
            act.wait_ge(tables_ready, 1)
            pairs = act.value_load(loops_i[0:1, 0:1], min_val=1, max_val=TILES // 2)
            with act.Fori(0, pairs) as g:
                for u in range(2):
                    t = 2 * g + u

                    def exp_k(half):
                        act.wait_ge(proj_read, 4 + 4 * t + half + 1)
                        act.wait_ge(kv_ready, 2 * t + half + 1)
                        e = slice(half * BLOCK, (half + 1) * BLOCK)
                        nc.scalar.activation(k_exp[:, e], k_raw[:, e], ACT.Exp)
                        nc.scalar.activation(k_raw[:, e], k_raw[:, e], ACT.Relu).then_inc(kexp_ready, 1)

                    exp_k(0)
                    at = act.value_load(start_i[0:1, ds(t + 2, 1)], min_val=0, max_val=SLOTS)
                    for s in (0, 2):
                        act.wait_ge(stage_done, 5 * t + 4 + 1 + s + 1)
                        apart(act)
                        read_selected(copy, 1 - u, s, 2 + (u + 1 + s) % 2, ds(at, P), stage_act)
                        if s == 0:
                            exp_k(1)
                    act.wait_ge(kx_ready, t + 3)
                    nc.scalar.activation(x_hl[u][:, HI, :], x_in[u], ACT.Copy, scale=XS).then_inc(kxhi_ready, 1)
                    for half in range(2):
                        act.wait_ge(kv_ready, 2 + 2 * t + half + 1)
                        e = slice(half * BLOCK, (half + 1) * BLOCK)
                        nc.scalar.activation(kv_hl[:, HI, e], v_raw[:, e], ACT.Copy, scale=KVS).then_inc(kvhi_ready, 1)

            def piece_hi(grp, par, q):
                act.wait_ge(w_loaded[q % 2], 16 * (2 * grp + q // 2 + 1))
                nc.scalar.activation(ring[par][:, q, HI, :], stage[q % 2][:, :], ACT.Copy, scale=WS)\
                  .then_inc(whi_ready, 1)

            for q in range(PIECES):
                piece_hi(0, 0, q)
            act.wait_ge(scaled, 1)
            nc.scalar.activation(logits[:, :, :], logits[:, :, :], ACT.Exp)
            nc.scalar.activation(prob[:, :, :], prob[:, :, :], ACT.Exp).then_inc(probs_ready, 1)
            act.wait_ge(sums_done, 1)
            act.wait_ge(sums_stored, 1)

            def group_steps(grp, par, attention, last=False):
                for j in range(BLOCKS):
                    s = BLOCKS * grp + j
                    for f in range(FT):
                        act.wait_ge(up_done, FT * s + f + 1)
                        act.wait_ge(hlo_ready, FT * s + f + 1)
                        apart(act)
                        src = out_bank(FT * (j % 2) + f)
                        if attention:
                            bias = bq_c[:, ds(FT * grp + f, 1)]
                            nc.scalar.activation(q_exp[f], src, ACT.Exp, bias=bias, scale=INV_XW)
                            nc.scalar.activation(h_f32[f], src, ACT.Relu, bias=bias, scale=INV_XW).then_inc(up_read, 1)
                        else:
                            bias = b1_c[:, ds(FT * (grp - ATT_GROUPS) + f, 1)]
                            nc.scalar.activation(h_f32[f], src, ACT.Gelu, bias=bias, scale=INV_XW).then_inc(up_read, 1)
                    for f in range(FT):
                        if attention:
                            act.wait_ge(ctx_ready, FT * s + f + 1 + FT)
                        else:
                            act.wait_ge(up_read, 4 + FT * s + f + 1)
                        act.wait_ge(down_done, 8 * s + 8)
                        nc.scalar.activation(h_hl[j % 2][:, f, HI, :], h_f32[f], ACT.Copy,
                                             scale=1.0 if attention else HS).then_inc(hhi_ready, 1)
                    if last:
                        if j >= 1:
                            gates(j - 1)
                        continue
                    if j >= 2:
                        act.wait_ge(down_done, 8 * s)
                    piece_hi(grp + 1, 1 - par, j)

            with act.Fori(0, ATT_GROUPS // 2) as g:
                for v in range(2):
                    group_steps(2 * g + v, v, True)
            def gates(b):
                for k in range(BLOCK // P):
                    st = b * (BLOCK // P) + k
                    act.wait_ge(down_added, 4 + 8 * (STEPS - BLOCKS + b) + 2 * (k + 1))
                    if st >= 2:
                        act.wait_ge(fin_ready, st - 1)
                    nc.scalar.activation(fg[st % 2], acc[:, st, :], ACT.Silu,
                                         scale=meta_s[:, st, 1:2].bitcast(F32)).then_inc(g_ready, 1)

            with act.Fori(0, FFN_GROUPS // 2 - 1) as g:
                for v in range(2):
                    group_steps(ATT_GROUPS + 2 * g + v, v, False)
            group_steps(GROUPS - 2, 0, False)
            act.wait_ge(meta_loaded, 16)
            act.wait_ge(acc_ready, 2 * BLOCKS)
            group_steps(GROUPS - 1, 1, False, last=True)
            gates(BLOCKS - 1)

        @block.vector
        def _(dve):
            scratch = [small[:, 0, n:n + 1] for n in range(TILES)]
            for i, (s, n) in enumerate(((proj_read, 4), (win_stored, 32), (tail_stored, 16),
                         (kv_ready, 2), (up_read, 4), (down_done, 16), (down_added, 4), (hlo_ready, FT),
                         (ctx_ready, FT))):
                nc.vector.memset(scratch[i], 0.0).then_inc(s, n)
            dve.wait_ge(const_ready, 1)
            nc.vector.tensor_copy(iota[:, :], iota_i)
            nc.vector.tensor_copy(ident_f, ident[:, 0:EXPERTS + 1]).then_inc(ident_ready, 1)

            def stats_x(u, n, loaded):
                dve.wait_ge(kx_loaded[u], loaded)
                for half in range(2):
                    ins = nc.vector.bn_stats(bn[u][:, half, :], x_in[u][:, half * 512:(half + 1) * 512])
                ins.then_inc(stats_ready, 1)
                dve.wait_ge(stats_ready, n)
                apart(dve)
                nc.vector.bn_aggr(mv[u][:, :], bn[u][:, :, :].rearrange("p a b -> p (a b)")).then_inc(var_ready, 1)

            def norm_x(u, col, n):
                dve.wait_ge(rstd_ready, n)
                nc.vector.tensor_copy(rstd_t[:, ds(col, 1)], rstd[u][:, :])
                nc.vector.tensor_scalar(x_in[u], x_in[u], mv[u][:, 0:1], rstd[u][:, :],
                                        ALU.subtract, ALU.mult).then_inc(kx_ready, 1)

            def low_x(u, n):
                dve.wait_ge(kxhi_ready, n)
                nc.vector.scalar_tensor_tensor(x_hl[u][:, LO, :], x_in[u], XS, x_hl[u][:, HI, :],
                                               ALU.mult, ALU.subtract).then_inc(kxlo_ready, 1)

            for u in range(2):
                stats_x(u, u + 1, 16)
            for u in range(2):
                norm_x(u, u, u + 1)

            def low_wkv(q):
                dve.wait_ge(wkv_hi, q + 1)
                nc.vector.scalar_tensor_tensor(wkv[:, q, LO, :], (k_stage + v_stage)[q], WS, wkv[:, q, HI, :],
                                               ALU.mult, ALU.subtract).then_inc(wkv_ready, 1)

            for q in range(CH):
                low_wkv(q)

            own = Chain(dve, dve_route)
            dve.wait_ge(logits_done, TOKEN_BLOCKS)
            nc.vector.tensor_copy(sums_x[:, :, :].rearrange("p t e -> p (t e)"), bank[0][:, 0:TILES * (EXPERTS + 1)])
            own.link(nc.vector.tensor_scalar(rw_sum[:, :], bank[3][:, 0:EXPERTS], -1.0 / D, None, ALU.mult))
            for e in range(EXPERTS):
                ins = nc.vector.scalar_tensor_tensor(logits[:, :, e], sums_x[:, :, EXPERTS], rw_sum[:, e:e + 1],
                                                     sums_x[:, :, e], ALU.mult, ALU.add)
            own.link(ins)
            low_x(0, 1)
            low_x(1, 2)
            for t in range(TILES):
                ins = nc.vector.max(top_v[:, t, :], logits[:, t, :])
            own.link(ins)
            for t in range(TILES):
                ins = nc.vector.max_index(top_i[:, t, :], top_v[:, t, :], logits[:, t, :])
            own.link(ins)
            for k in range(TOPK):
                nc.vector.tensor_tensor(prob[:, k, :], top_v[:, :, k], top_v[:, :, 0], ALU.subtract)
            nc.vector.tensor_tensor(logits[:, :, :], logits[:, :, :],
                                    top_v[:, :, 0:1].to_broadcast((P, TILES, EXPERTS)), ALU.subtract)
            for k in range(TOPK):
                ins = nc.vector.tensor_copy(top_f[:, k, :], top_i[:, :, k])
            own.link(ins)
            for k in range(TOPK):
                for e in range(EXPERTS):
                    ins = nc.vector.tensor_scalar(chosen[:, k, e, :], top_f[:, k, :], float(e), None, ALU.is_equal)
            ins.then_inc(chosen_ready, 1)

            def flat4(a):
                return a[:, :, :, :].rearrange("p k e t -> p (k e t)")

            dve.wait_ge(places_ready, 1)
            own.link(nc.vector.tensor_copy(flat4(totals), out_bank(1)))
            own.link(nc.vector.tensor_tensor_scan(flat4(running), run_mask[:, :, :].rearrange("p a t -> p (a t)"),
                                                  flat4(totals), 0.0, ALU.mult, ALU.add))
            own.link(nc.vector.tensor_tensor(flat4(place), flat4(running), flat4(totals), ALU.subtract))
            own.link(nc.vector.tensor_tensor(flat4(place), flat4(place), out_bank(0), ALU.add))
            for e in range(EXPERTS):
                ins = nc.vector.tensor_scalar(place[:, 1, e, :], place[:, 1, e, :], running[:, 0, e, TILES - 1:TILES],
                                              None, ALU.add)
            own.link(ins)
            own.link(nc.vector.scalar_tensor_tensor(flat4(place), flat4(place), float(CAPACITY), flat4(chosen),
                                                    ALU.is_lt, ALU.mult))
            own.link(nc.vector.tensor_reduce(keep[:, :, :], place[:, :, :, :].rearrange("p k e t -> p k t e"),
                                             AX.X, ALU.add))
            kept = small[:, 1, :]
            own.link(nc.vector.tensor_tensor(kept, keep[:, 0, :], keep[:, 1, :], ALU.max))
            nc.vector.tensor_copy(kept_h[:, :], kept).then_inc(kept_ready, 1)
            dve.wait_ge(ranks_ready, 1)
            tile_kept, run_kept, start = small[:, 2, :], small[:, 3, :], small[:, 4, :]
            nc.vector.tensor_copy(rank[:, 0:TILES], bank[0][:, 0:TILES])
            own.link(nc.vector.tensor_copy(tile_kept, bank[1][:, 0:TILES]))
            own.link(nc.vector.tensor_tensor_scan(run_kept, run_mask[:, 0, :], tile_kept, 0.0, ALU.mult, ALU.add))
            own.link(nc.vector.tensor_tensor(start, run_kept, tile_kept, ALU.subtract))
            nc.vector.memset(start_i[:, 0:1], 0)
            nc.vector.tensor_copy(start_i[:, 1:TILES + 1], start)
            nc.vector.tensor_copy(start_i[:, TILES + 1:TILES + 2], run_kept[:, TILES - 1:TILES])
            own.link(nc.vector.tensor_tensor(start, start, rank[:, 0:TILES], ALU.add))
            own.link(nc.vector.scalar_tensor_tensor(start, start, -float(NO_ROW), kept, ALU.add, ALU.mult))
            own.link(nc.vector.tensor_scalar(start, start, float(NO_ROW), None, ALU.add))
            nc.vector.tensor_copy(slot_i[:, :], start)
            own.link(nc.vector.scalar_tensor_tensor(rank_kept[:, 0:TILES], rank[:, 0:TILES], 1.0, kept,
                                                    ALU.add, ALU.mult))
            own.link(nc.vector.tensor_scalar(rank_kept[:, 0:TILES], rank_kept[:, 0:TILES], -1.0, None, ALU.add))
            last_tile, count = small[:, 5, :], small[:, 6, :]
            own.link(nc.vector.scalar_tensor_tensor(last_tile, tile_kept, 0.0, iota[:, 1:TILES + 1],
                                                    ALU.is_gt, ALU.mult))
            own.link(nc.vector.tensor_reduce(loops_f[:, 0:1], last_tile, AX.X, ALU.max))
            own.link(nc.vector.tensor_scalar(count[:, 0:TILES // 2], iota[:, 0:TILES // 2], 2.0, loops_f[:, 0:1],
                                             ALU.mult, ALU.is_lt))
            own.link(nc.vector.tensor_reduce(loops_f[:, 0:1], count[:, 0:TILES // 2], AX.X, ALU.add))
            tail_starts = iota[:, 0:SLOT_TILES + 1]
            own.link(nc.vector.tensor_scalar(loops_f[:, 1:2], run_kept[:, TILES - 1:TILES], -1.0, float(SLOTS),
                                             ALU.mult, ALU.add))
            own.link(nc.vector.tensor_scalar(count[:, 0:SLOT_TILES + 1], tail_starts, float(P), loops_f[:, 1:2],
                                             ALU.mult, ALU.is_le))
            own.link(nc.vector.tensor_reduce(loops_f[:, 1:2], count[:, 0:SLOT_TILES + 1], AX.X, ALU.add))
            own.link(nc.vector.tensor_copy(loops_i[:, :], loops_f[:, :]))

            def kept_columns(u, col):
                nc.vector.tensor_scalar(select[u][:, 1, :], iota[:, :], rank_kept[:, ds(col, 1)], None, ALU.is_equal)

            nc.vector.memset(carry[:, :], 0.0).then_inc(win_ready, 1)
            nc.vector.memset(upto[1][:, :], 0.0)
            kept_columns(0, 0)
            kept_columns(1, 1)
            nc.vector.memset(scratch[30], 0.0).then_inc(tables_ready, 1)
            low_wkv(CH)
            dve.wait_ge(wkv_ready, CH + 1)
            nc.vector.memset(kv_hl[:, :, :], 0.0).then_inc(kvlo_ready, 2)

            for s in (1, 3):
                dve.wait_ge(stage_done, s + 1)
                read_selected(nc.vector.tensor_copy, 0, s, 3, slice(0, P), stage_dve)
            for q in range(CH + 1, 2 * CH):
                low_wkv(q)
            dve.wait_ge(wkv_ready, 2 * CH)
            dve.wait_ge(rows_loaded, 48)
            pairs = dve.value_load(loops_i[0:1, 0:1], min_val=1, max_val=TILES // 2)

            def sums(u, t, n):
                dve.wait_ge(stage_done, n + 1)
                dve.wait_ge(win_stored, 16 * t + 16)
                dve.wait_ge(win_ready, t + 1)
                w = window[u]
                for c in range(2):
                    ins = nc.vector.scalar_tensor_tensor(
                        w[:, 4 * c:4 * c + 4, :],
                        bank[2 + u][:, c * BLOCK:(c + 1) * BLOCK].rearrange("p (c s) -> p c s", c=4), 1.0 / KVS,
                        carry[:, 4 * c:4 * c + 4].unsqueeze(2).to_broadcast((P, 4, P)), ALU.mult, ALU.add)
                ins.then_inc(stage_dve, 1)
                dve.wait_ge(stage_dve, 3 * t + 3)
                nc.vector.tensor_scalar(carry[:, :], w[:, :, P - 1], go_on[:, ds(t, 1)], None, ALU.mult)\
                  .then_inc(win_ready, 1)

            with dve.Fori(0, pairs) as g:
                for u in range(2):
                    t = 2 * g + u
                    e = [slice(h * BLOCK, (h + 1) * BLOCK) for h in range(2)]

                    def read_k(half):
                        dve.wait_ge(proj_done, 4 * t + half + 1)
                        nc.vector.scalar_tensor_tensor(k_raw[:, e[half]], out_bank(half), INV_XW, bk_row[:, e[half]],
                                                       ALU.mult, ALU.add).then_inc(proj_read, 1)

                    read_k(0)
                    sums(u, t, 5 * t + 4)
                    at = dve.value_load(start_i[0:1, ds(t + 2, 1)], min_val=0, max_val=SLOTS)

                    def read_odd(s):
                        dve.wait_ge(stage_done, 5 * t + 4 + 1 + s + 1)
                        read_selected(nc.vector.tensor_copy, 1 - u, s, 2 + (u + 1 + s) % 2, ds(at, P), stage_dve)

                    stats_x(u, t + 3, 16 * g + 32)
                    read_k(1)
                    read_odd(1)
                    norm_x(u, t + 2, t + 3)
                    kept_columns(u, t + 2)
                    nc.vector.tensor_scalar(upto[u][:, :], iota[:, :], rank[:, ds(t, 1)], None, ALU.is_ge)
                    for half in range(2):
                        dve.wait_ge(kexp_ready, 2 * t + half + 1)
                        ins = nc.vector.scalar_tensor_tensor(k_exp[:, e[half]], k_exp[:, e[half]], 1.0,
                                                             k_raw[:, e[half]], ALU.min, ALU.add)
                        ins.then_inc(phik_ready, 1)
                    low_x(u, t + 3)
                    for half in range(2):
                        dve.wait_ge(proj_done, 4 * t + 2 + half + 1)
                        own_v = nc.vector.scalar_tensor_tensor(v_raw[:, e[half]], out_bank(2 + half), INV_XW,
                                                               bv_row[:, e[half]], ALU.mult, ALU.add)
                        own_v.then_inc(proj_read, 1)
                        dve.wait_ge(proj_read, 4 + 4 * t + 2 + half + 1)
                        dve.wait_ge(phik_ready, 2 * t + half + 1)
                        nc.vector.tensor_tensor(v_raw[:, e[half]], v_raw[:, e[half]], k_exp[:, e[half]], ALU.mult)\
                          .then_inc(kv_ready, 1)
                        if half == 0:
                            read_odd(3)
                    for half in range(2):
                        dve.wait_ge(kvhi_ready, 2 * t + half + 1)
                        ins = nc.vector.scalar_tensor_tensor(kv_hl[:, LO, e[half]], v_raw[:, e[half]], KVS,
                                                             kv_hl[:, HI, e[half]], ALU.mult, ALU.subtract)
                        ins.then_inc(kvlo_ready, 1)
            kept = dve.value_load(start_i[0:1, TILES + 1:TILES + 2], min_val=0, max_val=SLOTS)
            tails = dve.value_load(loops_i[0:1, 1:2], min_val=1, max_val=SLOT_TILES + 1)
            with dve.Fori(0, tails) as n:
                at = nc.s_assert_within(kept + n * P, 0, SLOTS)
                nc.vector.tensor_copy(xnT[:, :, :, :].rearrange("p h c s -> p (h c) s")[:, :, ds(at, P)],
                                      zero_c[:, :].unsqueeze(2).to_broadcast((P, 2 * CH, P)))

            def piece_lo(grp, par, q):
                dve.wait_ge(whi_ready, PIECES * grp + q + 1)
                nc.vector.scalar_tensor_tensor(ring[par][:, q, LO, :], stage[q % 2][:, :], WS, ring[par][:, q, HI, :],
                                               ALU.mult, ALU.subtract).then_inc(wlo_ready, 1)

            for q in range(2):
                piece_lo(0, 0, q)
            last = 2 * pairs
            sums(0, last, 10 * pairs + 4)
            nc.vector.memset(scratch[31], 0.0).then_inc(sums_done, 1)

            for q in range(2, PIECES):
                piece_lo(0, 0, q)
            own = Chain(dve, dve_weights)
            nc.vector.tensor_tensor(prob[:, :, :], prob[:, :, :],
                                    rstd_t[:, 0:TILES].unsqueeze(1).to_broadcast((P, TOPK, TILES)), ALU.mult)
            nc.vector.tensor_tensor(logits[:, :, :], logits[:, :, :],
                                    rstd_t[:, 0:TILES].unsqueeze(2).to_broadcast((P, TILES, EXPERTS)), ALU.mult)\
              .then_inc(scaled, 1)
            dve.wait_ge(probs_ready, 1)
            own.link(nc.vector.tensor_reduce(z[:, :], logits[:, :, :], AX.X, ALU.add))
            own.link(nc.vector.reciprocal(z[:, :], z[:, :]))
            own.link(nc.vector.tensor_tensor(prob[:, :, :], prob[:, :, :], keep[:, :, :], ALU.mult))
            own.link(nc.vector.tensor_tensor(prob[:, 0, :], prob[:, 0, :], prob[:, 1, :], ALU.add))
            nc.vector.tensor_tensor(meta[:, :, 1].bitcast(F32), prob[:, 0, :], z[:, :], ALU.mult).then_inc(meta_ready, 1)

            def low_h(s, j, attention):
                for f in range(FT):
                    dve.wait_ge(hhi_ready, FT * s + f + 1)
                    nc.vector.scalar_tensor_tensor(h_hl[j % 2][:, f, LO, :], h_f32[f], 1.0 if attention else HS,
                                                   h_hl[j % 2][:, f, HI, :], ALU.mult, ALU.subtract).then_inc(hlo_ready, 1)

            def add_down(s, j, factor, start_count, then=None):
                dve.wait_ge(acc_ready, start_count)
                for m in range(8):
                    dve.wait_ge(down_done, 16 + 8 * s + m + 1)
                    row = acc[:, 4 * (j % BLOCKS) + m // 2, (m % 2) * BLOCK:(m % 2 + 1) * BLOCK]
                    nc.vector.scalar_tensor_tensor(row, out_bank(4 + m % 4), factor, row, ALU.mult, ALU.add)\
                      .then_inc(down_added, 1)
                    if then is not None and m % 2 and m >= 3:
                        then(m // 2 - 1)

            def result(st):
                u = st % 2
                dve.wait_ge(g_ready, st + 1)
                dve.wait_ge(fs_loaded[u], 16 * (st // 2 + 1))
                nc.vector.tensor_tensor(fs[u], fs[u], fg[u], ALU.mult).then_inc(gated_ready, 1)
                dve.wait_ge(gated_ready, st + 1)
                dve.wait_ge(fx_loaded[st % FX], 16 * (st // FX + 1))
                nc.vector.tensor_tensor(fx[st % FX], fx[st % FX], fs[u], ALU.add).then_inc(fin_ready, 1)

            def contexts(s, grp, j):
                for f in range(FT):
                    dve.wait_ge(up_read, 4 + FT * s + f + 1)
                    nc.vector.scalar_tensor_tensor(h_f32[f], q_exp[f], 1.0, h_f32[f], ALU.min, ALU.add).then_inc(phi_ready, 1)
                for f in range(FT):
                    dve.wait_ge(phi_ready, FT * s + f + 1)
                    dve.wait_ge(kvq_loaded[f], 16 * s + 16)
                    nc.vector.scalar_tensor_tensor(h_f32[f], h_f32[f], SCALE * CS, kvq[f], ALU.mult, ALU.mult)\
                      .then_inc(ctx_ready, 1)

            def body(base_group, attention, factor, count_at, last=False):
                n = 2 * BLOCKS
                for j in range(n + 1):
                    if j < n:
                        s = BLOCKS * base_group + j
                        grp = base_group + j // BLOCKS
                        if attention:
                            contexts(s, grp, j)
                        low_h(s, j, attention)
                        if not (last and j >= BLOCKS):
                            piece_lo(grp + 1, 1 - j // BLOCKS, j % BLOCKS)
                    if j >= 1:
                        b = (j - 1) % BLOCKS
                        tile = (BLOCK // P) * b
                        now = last and j == n
                        add_down(BLOCKS * base_group + j - 1, j - 1, factor, count_at(b),
                                 (lambda k: result(SLOT_TILES - BLOCK // P + k)) if now else None)
                        if last and j > BLOCKS:
                            for k in range(BLOCK // P - 1 if now else 0, BLOCK // P):
                                result(tile + k)

            with dve.Fori(0, ATT_GROUPS // 2) as g:
                body(2 * g, True, 1.0 / (CS * WS), lambda b: b + 1)
            with dve.Fori(0, FFN_GROUPS // 2 - 1) as g:
                body(ATT_GROUPS + 2 * g, False, 1.0 / (HS * WS), lambda b: BLOCKS + b + 1)
            body(GROUPS - 2, False, 1.0 / (HS * WS), lambda b: BLOCKS + b + 1, last=True)

        @block.tensor
        def _(pe):
            mm = nc.tensor.matmul
            pe.wait_ge(const_ready, 1)
            pe.wait_ge(params_loaded, 16 * PARAM_LOADS)

            for c in range(CH):
                mm(bank[3][:, 0:EXPERTS], ones_f, rw_f[:, c, 0:EXPERTS], start=(c == 0), stop=(c == CH - 1))
            pe.wait_ge(ident_ready, 1)
            with pe.Fori(0, TOKEN_BLOCKS // 2) as g:
                for u in range(2):
                    b = 2 * g + u
                    pe.wait_ge(xt_loaded[u], 16 * g + 16)
                    for c in range(CH):
                        ins = mm(scores(u), rw_f[:, c, :], xt_in[u][:, c, :], start=(c == 0), stop=(c == CH - 1))
                    ins.then_inc(scores_done, 1)
                for u in range(2):
                    b = 2 * g + u
                    pe.wait_ge(scores_read, b + 1)
                    for i in range(BLOCK // P):
                        ins = mm(bank[0][:, ds((BLOCK // P * b + i) * (EXPERTS + 1), EXPERTS + 1)],
                                 by_expert[u][0:EXPERTS + 1, i * P:(i + 1) * P], ident_f[0:EXPERTS + 1, :],
                                 start=True, stop=True)
                    ins.then_inc(logits_done, 1)

            pe.wait_ge(chosen_ready, 1)
            picks = chosen[:, :, :, :].rearrange("p k e t -> p (k e t)")
            mm(out_bank(0), before[:, :], picks, start=True, stop=True)
            mm(out_bank(1), ones[:, :], picks, start=True, stop=True).then_inc(places_ready, 1)
            pe.wait_ge(kept_ready, 1)
            mm(bank[0][:, 0:TILES], before[:, :], kept_h[:, :], start=True, stop=True)
            mm(bank[1][:, 0:TILES], ones[:, :], kept_h[:, :], start=True, stop=True).then_inc(ranks_ready, 1)

            def select_x(u, s, pair):
                for c in range(4):
                    cc = 4 * (s % 2) + c
                    ins = mm(bank[pair][:, c * 2 * P:(c + 1) * 2 * P], x_hl[u][:, s // 2, cc * P:(cc + 1) * P],
                             select[u][:, :, :].rearrange("p w t -> p (w t)"), start=True, stop=True)
                ins.then_inc(stage_done, 1)

            pe.wait_ge(tables_ready, 1)
            pe.wait_ge(kxlo_ready, 1)
            for s in range(4):
                if s >= 2:
                    pe.wait_ge((stage_act, stage_dve)[s % 2], 1)
                select_x(0, s, 2 + s % 2)
            pe.wait_ge(wkv_ready, CH)
            pairs = pe.value_load(loops_i[0:1, 0:1], min_val=1, max_val=TILES // 2)

            def project(u, t, n):
                pe.wait_ge(proj_read, 4 * t + n + 1)
                e = slice((n % 2) * BLOCK, (n % 2 + 1) * BLOCK)
                k = 0
                for c in range(CH):
                    for a, b in PASSES:
                        ins = mm(out_bank(n), xT[u][:, a, c, :], wkv[:, (n // 2) * CH + c, b, e],
                                 start=(k == 0), stop=(k == 3 * CH - 1))
                        k += 1
                ins.then_inc(proj_done, 1)

            def sum_kv(u, par, n):
                for c in range(CH):
                    for h in (HI, LO):
                        ins = mm(bank[2 + u][:, c * P:(c + 1) * P], kv_hl[:, h, c * P:(c + 1) * P], upto[par][:, :],
                                 start=(h == HI), stop=(h == LO))
                ins.then_inc(stage_done, 1)

            with pe.Fori(0, pairs) as g:
                for u in range(2):
                    t = 2 * g + u
                    pe.wait_ge(stage_act, 2 * t + 2)
                    pe.wait_ge(stage_dve, 3 * t + 2)
                    project(u, t, 0)
                    pe.wait_ge(kvlo_ready, 2 * t + 2)
                    sum_kv(u, 1 - u, 5 * t + 4)
                    pe.wait_ge(kxlo_ready, t + 2)
                    for s in range(4):
                        if s == 1:
                            project(u, t, 1)
                            pe.wait_ge(stage_dve, 3 * t + 3)
                        if s == 2:
                            pe.wait_ge(stage_act, 2 * t + 3)
                        if s == 3:
                            pe.wait_ge(wkv_ready, 2 * CH)
                            project(u, t, 2)
                            pe.wait_ge(stage_dve, 3 * t + 4)
                        select_x(1 - u, s, 2 + (u + 1 + s) % 2)
                    project(u, t, 3)
            pe.wait_ge(kvlo_ready, 4 * pairs + 2)
            pe.wait_ge(stage_dve, 6 * pairs + 2)
            pe.wait_ge(stage_act, 4 * pairs + 2)
            sum_kv(0, 1, 10 * pairs + 4)

            def up(s, j, grp, par):
                pe.wait_ge(wlo_ready, PIECES * grp + 2)
                for f in range(FT):
                    pe.wait_ge(up_read, FT * s + f + 1)
                    k = 0
                    for c in range(CH):
                        w = ring[par][:, c // 4, :, :].rearrange("p h (c n) -> p h c n", c=4)
                        for a, b in PASSES:
                            ins = mm(out_bank(FT * (j % 2) + f), w[:, a, c % 4, f * P:(f + 1) * P],
                                     xnT[:, b, c, (j % BLOCKS) * BLOCK:(j % BLOCKS + 1) * BLOCK],
                                     start=(k == 0), stop=(k == 3 * CH - 1))
                            k += 1
                    ins.then_inc(up_done, 1)

            def down(s, j, grp, par):
                pe.wait_ge(wlo_ready, PIECES * grp + PIECES)
                pe.wait_ge(hlo_ready, FT * s + FT + FT)
                for m in range(8):
                    pe.wait_ge(down_added, 8 * s + m + 1)
                    k = 0
                    for f in range(FT):
                        for a, b in PASSES:
                            ins = mm(out_bank(4 + m % 4), h_hl[j % 2][:, f, a, (m // 2) * P:(m // 2 + 1) * P],
                                     ring[par][:, 2 + f, b, (m % 2) * BLOCK:(m % 2 + 1) * BLOCK],
                                     start=(k == 0), stop=(k == 3 * FT - 1))
                            k += 1
                    ins.then_inc(down_done, 1)

            def body(base_group):
                n = 2 * BLOCKS
                for j in range(n + 1):
                    if j < n:
                        up(BLOCKS * base_group + j, j, base_group + j // BLOCKS, j // BLOCKS)
                    if j >= 1:
                        down(BLOCKS * base_group + j - 1, j - 1, base_group + (j - 1) // BLOCKS, (j - 1) // BLOCKS)

            with pe.Fori(0, GROUPS // 2) as g:
                body(2 * g)


_OUTS = [((4, 1024, 1024), "float32")]


def kernel(L0_attn_x, L0_attn_Wq, L0_attn_bq, L0_attn_Wk, L0_attn_bk, L0_attn_Wv, L0_attn_bv, L0_attn_Wo,
           L0_attn_bo, L0_ffn_router_w, L0_ffn_w1, L0_ffn_b1, L0_ffn_w2, L0_ffn_b2):
    import concourse.bacc as bacc
    from concourse.bass_utils import run_bass_kernel_spmd

    def rows_in(w):
        return np.asarray(w).T.reshape(-1, P, w.shape[0])

    def groups(up, down, n):
        a = rows_in(up).reshape(CH, P, n, GF).transpose(2, 1, 0, 3).reshape(n, P, 2, 1024)
        b = rows_in(down).reshape(n, FT, P, D).transpose(0, 2, 1, 3)
        return np.concatenate([a, b], axis=2)

    def columns(b):
        return np.asarray(b).reshape(-1, P).T

    arrays = {
        "x": np.asarray(L0_attn_x).reshape(TOKENS, D),
        "x_t": np.asarray(L0_attn_x).reshape(TOKEN_BLOCKS, BLOCK, CH, P).transpose(0, 3, 2, 1),
        "w_kv": np.concatenate([rows_in(L0_attn_Wk), rows_in(L0_attn_Wv)]),
        "router": rows_in(L0_ffn_router_w).transpose(1, 0, 2),
        "w_groups": np.concatenate([groups(L0_attn_Wq, L0_attn_Wo, ATT_GROUPS),
                                    groups(L0_ffn_w1, L0_ffn_w2, FFN_GROUPS)]),
        "b_k": np.asarray(L0_attn_bk).reshape(1, D), "b_v": np.asarray(L0_attn_bv).reshape(1, D),
        "b_q": columns(L0_attn_bq), "b_o": np.asarray(L0_attn_bo).reshape(1, D),
        "b_1": columns(L0_ffn_b1), "b_2": np.asarray(L0_ffn_b2).reshape(1, D),
    }
    arrays = {n: np.ascontiguousarray(a) for n, a in arrays.items()}
    nc = bacc.Bacc("TRN2", target_bir_lowering=False, num_devices=1)
    args = [nc.dram_tensor(n, a.shape, F32, kind="ExternalInput").ap() for n, a in arrays.items()]
    out = nc.dram_tensor("out", (TOKENS, D), F32, kind="ExternalOutput").ap()
    build(nc, *args, out)
    r = run_bass_kernel_spmd(nc, [arrays], core_ids=[0])
    return r.results[0]["out"].reshape(4, 1024, 1024)
```

```python
from contextlib import ExitStack

import numpy as np
import concourse.bass as bass
from concourse import mybir

F32 = mybir.dt.float32
F16 = mybir.dt.float16
I32 = mybir.dt.int32
U32 = mybir.dt.uint32
ALU = mybir.AluOpType
ACT = mybir.ActivationFunctionType
AX = mybir.AxisListType
ds = bass.ds

P = 128
TOKENS, D, F = 4096, 1024, 4096
SEQ = 1024
EXPERTS, TOPK, CAPACITY = 8, 2, 256
HEAD_DIM = 64
SCALE = HEAD_DIM ** -0.5
EPS = 1e-5

TILES = TOKENS // P
TOKEN_BLOCKS = TOKENS // 512
SEQ_TILES = SEQ // P
CH = D // P
SLOTS = EXPERTS * CAPACITY
SLOT_TILES = SLOTS // P
BLOCK = 512
BLOCKS = SLOTS // BLOCK
WIDE = SLOTS + P
GF = 256
FT = GF // P
ATT_GROUPS = D // GF
FFN_GROUPS = F // GF
GROUPS = ATT_GROUPS + FFN_GROUPS
PIECES = 4
NO_ROW = 8192

XS, WS, KVS, CS, HS = 2.0 ** 5, 2.0 ** 8, 2.0 ** 4, 2.0 ** 2, 2.0 ** 4

HI, LO = 0, 1
PASSES = ((HI, HI), (HI, LO), (LO, HI))


class Chain:

    def __init__(self, eng, sem, base=0):
        self.eng, self.sem, self.base, self.n = eng, sem, base, 0

    def step(self, ins):
        ins.then_inc(self.sem, 1)
        self.n += 1

    def wait(self):
        self.eng.wait_ge(self.sem, self.base + self.n)

    def link(self, ins):
        self.step(ins)
        self.wait()


def apart(eng):
    eng.nop(nofuse=True)


def build(nc, x, x_t, w_kv, router, w_groups, b_k, b_v, b_q, b_o, b_1, b_2, out):
    kvs_dram = nc.dram_tensor("kvs_dram", (CH, P, WIDE), F32, kind="Internal").ap()
    s_dram = nc.dram_tensor("s_dram", (SLOT_TILES, P, D), F32, kind="Internal").ap()
    meta_dram = nc.dram_tensor("meta_dram", (SLOTS, 2), I32, kind="Internal").ap()

    x_tiles = x.rearrange("(t p) d -> t p d", p=P)
    win_dram = kvs_dram.rearrange("c p s -> p c s")

    with ExitStack() as ctx:
        def sb(name, shape, dt):
            return ctx.enter_context(nc.sbuf_tensor(name, shape, dt))

        def sem(name):
            return ctx.enter_context(nc.semaphore(name))

        arena_a = sb("arena_a", [P, SLOT_TILES * D], F32)
        wkv = arena_a[:, :].bitcast(F16).rearrange("p (q h e) -> p q h e", q=2 * CH, h=2)
        acc = arena_a[:, :].rearrange("p (t e) -> p t e", t=SLOT_TILES)
        xnT = sb("xnT", [P, 2, CH, WIDE], F16)
        AR = 14 * 1024
        arena_b = sb("arena_b", [P, AR], F32)

        def part(at, n):
            return arena_b[:, at * 1024:at * 1024 + n * 1024]

        x_in = [part(u, 1) for u in range(2)]
        x_hl = [part(2 + u, 1).bitcast(F16).rearrange("p (h d) -> p h d", h=2) for u in range(2)]
        xT = [part(4 + u, 1).bitcast(F16).rearrange("p (h c t) -> p h c t", h=2, c=CH) for u in range(2)]
        k_raw, k_exp, v_raw = part(6, 1), part(7, 1), part(8, 1)
        kv_hl = part(9, 1).bitcast(F16).rearrange("p (h e) -> p h e", h=2)
        window = [part(10 + u, 1).rearrange("p (c s) -> p c s", c=CH) for u in range(2)]
        bk_row, bv_row = part(12, 1), part(13, 1)

        ring = [part(4 * u, 4).bitcast(F16).rearrange("p (q h e) -> p q h e", q=PIECES, h=2)
                for u in range(2)]
        h_f32 = [arena_b[:, 8 * 1024 + BLOCK * f:8 * 1024 + BLOCK * (f + 1)] for f in range(FT)]
        h_hl = [part(9 + u, 1).bitcast(F16).rearrange("p (f h s) -> p f h s", f=FT, h=2) for u in range(2)]
        kvq = [arena_b[:, 11 * 1024 + BLOCK * f:11 * 1024 + BLOCK * (f + 1)] for f in range(FT)]
        q_exp = [arena_b[:, 12 * 1024 + BLOCK * f:12 * 1024 + BLOCK * (f + 1)] for f in range(FT)]
        xnT_f = xnT[:, :, :, :].rearrange("p h c s -> p (h c s)").bitcast(F32)

        def table(at, name_dims, **dims):
            n = int(np.prod(list(dims.values())))
            at += 1024 * CH
            return xnT_f[:, at:at + n].rearrange(name_dims, **dims)

        N4 = TOPK * EXPERTS * TILES
        by_choice = dict(k=TOPK, e=EXPERTS, t=TILES)
        totals = table(0, "p (k e t) -> p k e t", **by_choice)
        running = table(N4, "p (k e t) -> p k e t", **by_choice)
        place = table(2 * N4, "p (k e t) -> p k e t", **by_choice)
        run_mask = table(3 * N4, "p (a t) -> p a t", a=TOPK * EXPERTS, t=TILES)
        top_v = table(4 * N4, "p (t e) -> p t e", t=TILES, e=EXPERTS)
        top_i = table(4 * N4 + 256, "p (t e) -> p t e", t=TILES, e=EXPERTS).bitcast(U32)
        chosen = xnT_f[:, 1024 * CH + 4 * N4 + 512:1024 * CH + 4 * N4 + 768].bitcast(F16)\
            .rearrange("p (k e t) -> p k e t", **by_choice)
        sums_x = table(4 * N4 + 768, "p (t e) -> p t e", t=TILES, e=EXPERTS + 1)
        iota_i = xnT_f[:, 1024 * CH + 4 * N4 + 1100:1024 * CH + 4 * N4 + 1100 + P].bitcast(I32)
        ones_f = xnT_f[:, 1024 * CH + 4 * N4 + 1300:1024 * CH + 4 * N4 + 1300 + P]
        top_f = table(4 * N4 + 1500, "p (k t) -> p k t", k=TOPK, t=TILES)
        by_expert = [xnT_f[:, 12288 + BLOCK * u:12288 + BLOCK * (u + 1)] for u in range(2)]
        ident_f = xnT_f[:, 13312:13312 + EXPERTS + 1]
        xt_in = [part(2 + 4 * u, 4).rearrange("p (c t) -> p c t", c=CH) for u in range(2)]
        FS = 4
        fs = [part(i, 1) for i in range(FS)]
        fg = [part(11 + u, 1) for u in range(2)]

        stage = [sb(f"stage{u}", [P, 1024], F32) for u in range(2)]
        bias_row = sb("bias_row", [P, D], F32)
        EARLY = TOKEN_BLOCKS - 2
        later = [part(10, 1), part(11, 1), stage[0][:, :], stage[1][:, :]]
        kv_stage = ([xnT_f[:, 1024 * c:1024 * (c + 1)] for c in range(EARLY)] + later
                    + [part(9, 1), part(6, 1), part(7, 1), part(8, 1)] + later[:CH - EARLY])

        ident = sb("ident", [P, P], F16)
        before = sb("before", [P, P], F16)
        ones = sb("ones", [P, P], F16)
        iota = sb("iota", [P, P], F32)
        select = [sb(f"select{u}", [P, 2, P], F16) for u in range(2)]
        upto = [sb(f"upto{u}", [P, P], F16) for u in range(2)]
        rw_f = sb("rw_f", [P, CH, EXPERTS + 1], F32)
        rw_sum = sb("rw_sum", [P, EXPERTS], F32)
        logits = sb("logits", [P, TILES, EXPERTS], F32)
        bq_c = sb("bq_c", [P, CH], F32)
        b1_c = sb("b1_c", [P, F // P], F32)
        eps_c = sb("eps_c", [P, 1], F32)
        power_c = sb("power_c", [P, 1], F32)
        zero_c = sb("zero_c", [P, 1], F16)

        bn = [sb(f"bn{u}", [P, 2, 6], F32) for u in range(2)]
        mv = [sb(f"mv{u}", [P, 2], F32) for u in range(2)]
        var = [sb(f"var{u}", [P, 1], F32) for u in range(2)]
        rstd = [sb(f"rstd{u}", [P, 1], F32) for u in range(2)]
        rstd_t = sb("rstd_t", [P, TILES + 2], F32)
        keep = sb("keep", [P, TOPK, TILES], F32)
        prob = sb("prob", [P, TOPK, TILES], F32)
        z = sb("z", [P, TILES], F32)
        small = sb("small", [P, 8, TILES], F32)
        kept_h = sb("kept_h", [P, TILES], F16)
        rank = sb("rank", [P, TILES + 2], F32)
        rank_kept = sb("rank_kept", [P, TILES + 2], F32)
        slot_i = sb("slot_i", [P, TILES], I32)
        start_i = sb("start_i", [P, TILES + 2], I32)
        loops_f = sb("loops_f", [P, 2], F32)
        loops_i = sb("loops_i", [P, 2], I32)
        meta = sb("meta", [P, TILES, 2], I32)
        meta_s = sb("meta_s", [P, SLOT_TILES, 2], I32)
        go_on = sb("go_on", [P, TILES + 2], F32)
        carry = sb("carry", [P, CH], F32)

        bank = [ctx.enter_context(nc.psum_tensor(f"pair{i}", [P, 2 * BLOCK], F32)) for i in range(4)]

        def out_bank(i):
            return bank[i // 2][:, (i % 2) * BLOCK:(i % 2 + 1) * BLOCK]

        FIRST_PAIRS = (2, 3, 0, 1)

        sums_w_done = sem("sums_w_done")
        const_ready, ident_ready = sem("const_ready"), sem("ident_ready")
        router_loaded, biases_loaded = sem("router_loaded"), sem("biases_loaded")
        pool_consts = sem("pool_consts")
        xt_loaded = [sem(f"xt_loaded{u}") for u in range(2)]
        scores_done, scores_read, logits_done = sem("scores_done"), sem("scores_read"), sem("logits_done")
        logits_read = sem("logits_read")
        wkv_loaded = [sem(f"wkv_loaded{q}") for q in range(2 * CH)]
        wkv_hi, wkv_ready = sem("wkv_hi"), sem("wkv_ready")
        dve_route, dve_weights = sem("dve_route"), sem("dve_weights")
        scaled, probs_ready = sem("scaled"), sem("probs_ready")
        chosen_ready, places_ready = sem("chosen_ready"), sem("places_ready")
        kept_ready, ranks_ready = sem("kept_ready"), sem("ranks_ready")
        tables_ready, meta_ready, select_ready = sem("tables_ready"), sem("meta_ready"), sem("select_ready")
        meta_filled, meta_stored, meta_loaded = sem("meta_filled"), sem("meta_stored"), sem("meta_loaded")
        rows_loaded = sem("rows_loaded")
        kx_loaded = [sem(f"kx_loaded{u}") for u in range(2)]
        stats_ready, var_ready, var_eps, rstd_ready = (sem(n) for n in ("stats_ready", "var_ready", "var_eps", "rstd_ready"))
        kx_ready, kxhi_ready, kxlo_ready = sem("kx_ready"), sem("kxhi_ready"), sem("kxlo_ready")
        stage_done, stage_dve, stage_act = sem("stage_done"), sem("stage_dve"), sem("stage_act")
        proj_done, proj_read = sem("proj_done"), sem("proj_read")
        kexp_ready, phik_ready = sem("kexp_ready"), sem("phik_ready")
        kv_ready, kvhi_ready, kvlo_ready = sem("kv_ready"), sem("kvhi_ready"), sem("kvlo_ready")
        win_ready, win_stored = sem("win_ready"), sem("win_stored")
        tail_stored = sem("tail_stored")
        sums_done, sums_stored = sem("sums_done"), sem("sums_stored")
        w_loaded = [sem(f"w_loaded{u}") for u in range(2)]
        whi_ready, wlo_ready = sem("whi_ready"), sem("wlo_ready")
        kvq_loaded = [sem(f"kvq_loaded{f}") for f in range(FT)]
        up_done, up_read = sem("up_done"), sem("up_read")
        hhi_ready, hlo_ready = sem("hhi_ready"), sem("hlo_ready")
        phi_ready, ctx_ready = sem("phi_ready"), sem("ctx_ready")
        down_done, down_added = sem("down_done"), sem("down_added")
        acc_ready, s_stored, b2_loaded = sem("acc_ready"), sem("s_stored"), sem("b2_loaded")
        copied = sem("copied")
        g_ready, fin_ready = sem("g_ready"), sem("fin_ready")
        fin_stored = [sem(f"fin_stored{i}") for i in range(FS)]
        fs_loaded = [sem(f"fs_loaded{i}") for i in range(FS)]

        block = ctx.enter_context(nc.Block())

        INV_XW = 1.0 / (XS * WS)
        STEPS = BLOCKS * GROUPS

        def scores(u):
            return bank[2][0:EXPERTS + 1, u * BLOCK:(u + 1) * BLOCK]

        def by_token(u):
            n = (BLOCK // P) * (EXPERTS + 1)
            return bank[0][:, u * BLOCK:u * BLOCK + n].rearrange("p (t e) -> p t e", e=EXPERTS + 1)

        def read_selected(copy, u, s, pair, at, signal):
            c = slice(4 * (s % 2), 4 * (s % 2) + 4)
            both = bank[pair][:, :].rearrange("p (c w t) -> p c w t", c=4, w=2)
            copy(xT[u][:, s // 2, c, :], both[:, :, 0, :])
            copy(xnT[:, s // 2, c, at], both[:, :, 1, :]).then_inc(signal, 1)

        @block.sync
        def _(sp):
            sp.dma_start(rw_f[:, :, 0:EXPERTS], router).then_inc(router_loaded, 16)
            for b in range(TOKEN_BLOCKS):
                if b >= 2:
                    sp.wait_ge(scores_done, b - 1)
                sp.dma_start(xt_in[b % 2], x_t[b]).then_inc(xt_loaded[b % 2], 16)
                if b < EARLY:
                    sp.dma_start(kv_stage[b], w_kv[b]).then_inc(wkv_loaded[b], 16)
                if b == 1:
                    for u in range(2):
                        sp.dma_start(x_in[u], x_tiles[u]).then_inc(kx_loaded[u], 16)
            for q in range(EARLY, EARLY + 4):
                sp.dma_start(kv_stage[q], w_kv[q]).then_inc(wkv_loaded[q], 16)
            sp.wait_ge(scores_done, TOKEN_BLOCKS)
            for q in range(EARLY + 4, CH + EARLY):
                sp.dma_start(kv_stage[q], w_kv[q]).then_inc(wkv_loaded[q], 16)
            for row, src in ((bk_row, b_k), (bv_row, b_v), (bias_row[:, :], b_o)):
                sp.dma_start(row, src.to_broadcast((P, D))).then_inc(rows_loaded, 16)
            for q in range(CH + EARLY, 2 * CH):
                sp.wait_ge(wkv_ready, q - CH + 1)
                sp.dma_start(kv_stage[q], w_kv[q]).then_inc(wkv_loaded[q], 16)
            sp.dma_start(bq_c[:, :], b_q).then_inc(biases_loaded, 16)
            sp.dma_start(b1_c[:, :], b_1).then_inc(biases_loaded, 16)

            def piece(g, q):
                sp.dma_start(stage[q % 2][:, :], w_groups[g, :, q, :]).then_inc(w_loaded[q % 2], 16)

            sp.wait_ge(wkv_ready, 2 * CH)
            for q in range(2):
                piece(0, q)

            sp.wait_ge(tables_ready, 1)
            pairs = sp.value_load(loops_i[0:1, 0:1], min_val=1, max_val=TILES // 2)
            with sp.Fori(0, pairs) as g:
                for u in range(2):
                    t = 2 * g + u
                    sp.wait_ge(kxlo_ready, t + 1)
                    apart(sp)
                    sp.dma_start(x_in[u], x_tiles[(t + 2) % TILES]).then_inc(kx_loaded[u], 16)
                    at = sp.value_load(start_i[0:1, ds(t, 1)], min_val=0, max_val=SLOTS)
                    sp.wait_ge(win_ready, t + 2)
                    sp.wait_ge(win_stored, 16 * t + 32)
                    apart(sp)
                    sp.dma_start(win_dram[:, :, ds(at, P)], window[u]).then_inc(win_stored, 16)
            last = 2 * pairs
            at = sp.value_load(start_i[0:1, ds(last, 1)], min_val=0, max_val=SLOTS)
            sp.wait_ge(win_ready, last + 2)
            sp.wait_ge(win_stored, 16 * last + 32)
            apart(sp)
            sp.dma_start(win_dram[:, :, ds(at, P)], window[0]).then_inc(win_stored, 16)
            sp.wait_ge(win_stored, 16 * last + 48)
            apart(sp)
            kept = sp.value_load(start_i[0:1, TILES + 1:TILES + 2], min_val=0, max_val=SLOTS)
            tails = sp.value_load(loops_i[0:1, 1:2], min_val=1, max_val=SLOT_TILES + 1)
            with sp.Fori(0, tails) as n:
                at = nc.s_assert_within(kept + n * P, 0, SLOTS)
                sp.wait_ge(tail_stored, 16 * n + 16)
                apart(sp)
                sp.dma_start(win_dram[:, :, ds(at, P)], window[0]).then_inc(tail_stored, 16)
            sp.wait_ge(tail_stored, 16 * tails + 16)
            sp.nop().then_inc(sums_stored, 1)

            for q in range(2, PIECES):
                sp.wait_ge(wlo_ready, q - 1)
                piece(0, q)
            sp.wait_ge(sums_done, 1)

            def copy_rows(n):
                rows = TOKENS // FFN_GROUPS
                sp.dma_start(out.rearrange("(n a r) d -> n a (r d)", n=FFN_GROUPS, a=16)[n],
                             x.rearrange("(n a r) d -> n a (r d)", n=FFN_GROUPS, a=16)[n]).then_inc(copied, 16)

            def group_steps(grp, attention):
                for j in range(BLOCKS):
                    if attention:
                        for f in range(FT):
                            sp.wait_ge(ctx_ready, FT * (BLOCKS * grp + j - 1) + f + 1 + FT)
                            sp.dma_start(kvq[f], kvs_dram[FT * grp + f, :, j * BLOCK:(j + 1) * BLOCK])\
                              .then_inc(kvq_loaded[f], 16)
                    sp.wait_ge(wlo_ready, PIECES * grp + PIECES + j - 1)
                    piece(grp + 1, j)

            with sp.Fori(0, ATT_GROUPS // 2) as g:
                for v in range(2):
                    group_steps(2 * g + v, True)
            with sp.Fori(0, FFN_GROUPS // 2 - 1) as g:
                for v in range(2):
                    copy_rows(2 * g + v)
                    group_steps(ATT_GROUPS + 2 * g + v, False)
            copy_rows(FFN_GROUPS - 2)
            copy_rows(FFN_GROUPS - 1)
            group_steps(GROUPS - 2, False)

            sp.wait_ge(down_done, 16 + 8 * (STEPS - BLOCKS))
            for st in range(SLOT_TILES):
                if st >= FS:
                    sp.wait_ge(fin_stored[st % FS], 16 * (st // FS))
                sp.dma_start(fs[st % FS], s_dram[st]).then_inc(fs_loaded[st % FS], 16)
            for i in range(FS):
                sp.wait_ge(fs_loaded[i], 16 * (SLOT_TILES // FS))

        @block.gpsimd
        def _(pool):
            ch = Chain(pool, pool_consts)
            nc.gpsimd.memset(ones[:, :], 1.0)
            nc.gpsimd.memset(ones_f, 1.0)
            nc.gpsimd.memset(rw_f[:, :, EXPERTS:EXPERTS + 1], 1.0)
            nc.gpsimd.memset(eps_c[:, :], EPS)
            nc.gpsimd.memset(power_c[:, :], -0.5)
            nc.gpsimd.memset(zero_c[:, :], 0.0)
            nc.gpsimd.memset(rstd_t[:, :], 0.0)
            nc.gpsimd.memset(rank[:, TILES:TILES + 2], 0.0)
            nc.gpsimd.memset(rank_kept[:, TILES:TILES + 2], -1.0)
            nc.gpsimd.memset(run_mask[:, :, :], 1.0)
            nc.gpsimd.memset(go_on[:, :], 1.0)
            nc.gpsimd.iota(iota_i, [[1, P]], base=0, channel_multiplier=0)
            nc.gpsimd.iota(meta[:, :, 0], [[P, TILES]], base=0, channel_multiplier=1)
            nc.gpsimd.memset(meta_s[:, :, 0], NO_ROW)
            nc.gpsimd.memset(meta_s[:, :, 1], 0)
            ch.link(nc.gpsimd.memset(ident[:, :], 0.0))
            for t in range(0, TILES + 2, SEQ_TILES):
                nc.gpsimd.memset(go_on[:, t:t + 1], 0.0)
            nc.gpsimd.memset(run_mask[:, :, 0:1], 0.0)
            nc.gpsimd.affine_select(out=before[:, :], in_=ones[:, :], pattern=[[1, P]], compare_op=ALU.is_gt,
                                    fill=0.0, base=0, channel_multiplier=-1)
            ch.link(nc.gpsimd.affine_select(out=ident[:, :], in_=ident[:, :], pattern=[[-1, P]],
                                            compare_op=ALU.not_equal, fill=1.0, base=0,
                                            channel_multiplier=1))
            for u in range(2):
                last = nc.gpsimd.tensor_copy(select[u][:, 0, :], ident[:, :])
            last.then_inc(const_ready, 1)
            pool.dma_start(meta_dram.rearrange("(t p) c -> p t c", p=P), meta_s[:, :, :]).then_inc(meta_filled, 16)

            def reciprocal_deviation(u, n):
                pool.wait_ge(var_ready, n)
                nc.gpsimd.tensor_tensor(var[u][:, :], mv[u][:, 1:2], eps_c[:, :], ALU.add).then_inc(var_eps, 1)
                pool.wait_ge(var_eps, n)
                nc.gpsimd.tensor_tensor(rstd[u][:, :], var[u][:, :], power_c[:, :], ALU.pow).then_inc(rstd_ready, 1)

            reciprocal_deviation(0, 1)
            reciprocal_deviation(1, 2)
            pool.wait_ge(wkv_ready, EARLY + 5)
            nc.gpsimd.memset(kv_hl[:, :, :], 0.0).then_inc(kvlo_ready, 2)
            pool.wait_ge(tables_ready, 1)
            pairs = pool.value_load(loops_i[0:1, 0:1], min_val=1, max_val=TILES // 2)
            with pool.Fori(0, pairs) as g:
                for u in range(2):
                    reciprocal_deviation(u, 2 * g + u + 3)

            pool.wait_ge(sums_done, 1)
            pool.wait_ge(rows_loaded, 48)
            for b in range(SLOT_TILES):
                ins = nc.gpsimd.tensor_copy(acc[:, b, :], bias_row[:, :])
                if b % BLOCKS == BLOCKS - 1:
                    ins.then_inc(acc_ready, 1)
            pool.wait_ge(meta_ready, 1)
            pool.wait_ge(meta_filled, 16)
            for t in range(TILES):
                pool.indirect_dma_start(
                    meta_dram, bass.IndirectOffsetOnAxis(ap=slot_i[:, t:t + 1].bitcast(U32), axis=0), meta[:, t, :], None,
                    bounds_check=SLOTS - 1, oob_is_err=False).then_inc(meta_stored, 16)
            pool.wait_ge(meta_stored, 16 * TILES)
            pool.dma_start(meta_s[:, :, :], meta_dram.rearrange("(t p) c -> p t c", p=P)).then_inc(meta_loaded, 16)

            pool.wait_ge(acc_ready, BLOCKS)
            pool.dma_start(bias_row[:, :], b_2.to_broadcast((P, D))).then_inc(b2_loaded, 16)
            pool.wait_ge(b2_loaded, 16)
            ATT_STEPS = ATT_GROUPS * BLOCKS
            for b in range(BLOCKS):
                pool.wait_ge(down_added, 4 + 8 * (ATT_STEPS - BLOCKS + b + 1))
                rows = slice(b * (BLOCK // P), (b + 1) * (BLOCK // P))
                pool.dma_start(s_dram[rows].rearrange("t p e -> p t e"), acc[:, rows, :]).then_inc(s_stored, 16)
                pool.wait_ge(s_stored, 16 * (b + 1))
                for st in range(b * (BLOCK // P), (b + 1) * (BLOCK // P)):
                    ins = nc.gpsimd.tensor_copy(acc[:, st, :], bias_row[:, :])
                ins.then_inc(acc_ready, 1)

            pool.wait_ge(meta_loaded, 16)
            pool.wait_ge(copied, 16 * FFN_GROUPS)

            for st in range(SLOT_TILES):
                pool.wait_ge(fin_ready, st + 1)
                pool.indirect_dma_start(
                    out, bass.IndirectOffsetOnAxis(ap=meta_s[:, st, 0:1].bitcast(U32), axis=0), fs[st % FS], None,
                    bounds_check=TOKENS - 1, oob_is_err=False, compute_op=ALU.add)\
                    .then_inc(fin_stored[st % FS], 16)
            for i in range(FS):
                pool.wait_ge(fin_stored[i], 16 * (SLOT_TILES // FS))

        @block.scalar
        def _(act):

            def high_wkv(q):
                act.wait_ge(wkv_loaded[q], 16)
                nc.scalar.activation(wkv[:, q, HI, :], kv_stage[q], ACT.Copy, scale=WS).then_inc(wkv_hi, 1)

            for b in range(TOKEN_BLOCKS):
                act.wait_ge(scores_done, b + 1)
                if b >= 2:
                    act.wait_ge(logits_done, b - 1)
                nc.scalar.activation(by_expert[b % 2][0:EXPERTS + 1, :], scores(b % 2), ACT.Copy).then_inc(scores_read, 1)
                if b < EARLY:
                    high_wkv(b)
            for u in range(2):
                act.wait_ge(kx_ready, u + 1)
                nc.scalar.activation(x_hl[u][:, HI, :], x_in[u], ACT.Copy, scale=XS).then_inc(kxhi_ready, 1)
            for q in range(EARLY, CH + EARLY):
                high_wkv(q)

            def copy(dst, src):
                return nc.scalar.activation(dst, src, ACT.Copy)

            act.wait_ge(tables_ready, 1)
            for s in (0, 2):
                act.wait_ge(stage_done, s + 1)
                read_selected(copy, 0, s, FIRST_PAIRS[s], slice(0, P), stage_act)
            for q in range(CH + EARLY, 2 * CH):
                high_wkv(q)
            pairs = act.value_load(loops_i[0:1, 0:1], min_val=1, max_val=TILES // 2)
            with act.Fori(0, pairs) as g:
                for u in range(2):
                    t = 2 * g + u

                    def exp_k(half):
                        act.wait_ge(proj_read, 4 + 4 * t + half + 1)
                        act.wait_ge(kv_ready, 2 * t + half + 1)
                        e = slice(half * BLOCK, (half + 1) * BLOCK)
                        nc.scalar.activation(k_exp[:, e], k_raw[:, e], ACT.Exp)
                        nc.scalar.activation(k_raw[:, e], k_raw[:, e], ACT.Relu).then_inc(kexp_ready, 1)

                    exp_k(0)
                    at = act.value_load(start_i[0:1, ds(t + 2, 1)], min_val=0, max_val=SLOTS)
                    for s in (0, 2):
                        act.wait_ge(stage_done, 5 * t + 4 + 1 + s + 1)
                        apart(act)
                        read_selected(copy, 1 - u, s, 2 + (u + 1 + s) % 2, ds(at, P), stage_act)
                        if s == 0:
                            exp_k(1)
                    act.wait_ge(kx_ready, t + 3)
                    nc.scalar.activation(x_hl[u][:, HI, :], x_in[u], ACT.Copy, scale=XS).then_inc(kxhi_ready, 1)
                    for half in range(2):
                        act.wait_ge(kv_ready, 2 + 2 * t + half + 1)
                        e = slice(half * BLOCK, (half + 1) * BLOCK)
                        nc.scalar.activation(kv_hl[:, HI, e], v_raw[:, e], ACT.Copy, scale=KVS).then_inc(kvhi_ready, 1)

            def piece_hi(grp, par, q):
                act.wait_ge(w_loaded[q % 2], 16 * (2 * grp + q // 2 + 1))
                nc.scalar.activation(ring[par][:, q, HI, :], stage[q % 2][:, :], ACT.Copy, scale=WS)\
                  .then_inc(whi_ready, 1)

            act.wait_ge(biases_loaded, 32)
            for q in range(PIECES):
                piece_hi(0, 0, q)
            act.wait_ge(scaled, 1)
            nc.scalar.activation(logits[:, :, :], logits[:, :, :], ACT.Exp)
            nc.scalar.activation(prob[:, :, :], prob[:, :, :], ACT.Exp).then_inc(probs_ready, 1)
            act.wait_ge(sums_done, 1)
            act.wait_ge(sums_stored, 1)

            def group_steps(grp, par, attention, last=False):
                for j in range(BLOCKS):
                    s = BLOCKS * grp + j
                    for f in range(FT):
                        act.wait_ge(up_done, FT * s + f + 1)
                        act.wait_ge(hlo_ready, FT * s + f + 1)
                        apart(act)
                        src = out_bank(FT * (j % 2) + f)
                        if attention:
                            bias = bq_c[:, ds(FT * grp + f, 1)]
                            nc.scalar.activation(q_exp[f], src, ACT.Exp, bias=bias, scale=INV_XW)
                            nc.scalar.activation(h_f32[f], src, ACT.Relu, bias=bias, scale=INV_XW).then_inc(up_read, 1)
                        else:
                            bias = b1_c[:, ds(FT * (grp - ATT_GROUPS) + f, 1)]
                            nc.scalar.activation(h_f32[f], src, ACT.Gelu, bias=bias, scale=INV_XW).then_inc(up_read, 1)
                    for f in range(FT):
                        if attention:
                            act.wait_ge(ctx_ready, FT * s + f + 1 + FT)
                        else:
                            act.wait_ge(up_read, 4 + FT * s + f + 1)
                        act.wait_ge(down_done, 8 * s + 8)
                        nc.scalar.activation(h_hl[j % 2][:, f, HI, :], h_f32[f], ACT.Copy,
                                             scale=1.0 if attention else HS).then_inc(hhi_ready, 1)
                    if last:
                        if j >= 1:
                            gates(j - 1)
                        continue
                    if j >= 2:
                        act.wait_ge(down_done, 8 * s)
                    piece_hi(grp + 1, 1 - par, j)

            with act.Fori(0, ATT_GROUPS // 2) as g:
                for v in range(2):
                    group_steps(2 * g + v, v, True)
            def gates(b):
                for k in range(BLOCK // P):
                    st = b * (BLOCK // P) + k
                    act.wait_ge(down_added, 4 + 8 * (STEPS - BLOCKS + b) + 2 * (k + 1))
                    if st >= 2:
                        act.wait_ge(fin_ready, st - 1)
                    nc.scalar.activation(fg[st % 2], acc[:, st, :], ACT.Silu,
                                         scale=meta_s[:, st, 1:2].bitcast(F32)).then_inc(g_ready, 1)

            with act.Fori(0, FFN_GROUPS // 2 - 1) as g:
                for v in range(2):
                    group_steps(ATT_GROUPS + 2 * g + v, v, False)
            group_steps(GROUPS - 2, 0, False)
            act.wait_ge(meta_loaded, 16)
            group_steps(GROUPS - 1, 1, False, last=True)
            gates(BLOCKS - 1)

        @block.vector
        def _(dve):
            scratch = [small[:, 0, n:n + 1] for n in range(TILES)]
            for i, (s, n) in enumerate(((logits_read, 2), (proj_read, 4), (win_stored, 32), (tail_stored, 16),
                         (kv_ready, 2), (up_read, 4), (down_done, 16), (down_added, 4), (hlo_ready, FT),
                         (ctx_ready, FT))):
                nc.vector.memset(scratch[i], 0.0).then_inc(s, n)
            dve.wait_ge(const_ready, 1)
            nc.vector.tensor_copy(iota[:, :], iota_i)
            nc.vector.tensor_copy(ident_f, ident[:, 0:EXPERTS + 1]).then_inc(ident_ready, 1)
            own = Chain(dve, dve_route)
            dve.wait_ge(sums_w_done, 1)
            own.link(nc.vector.tensor_scalar(rw_sum[:, :], bank[3][:, 0:EXPERTS], -1.0 / D, None, ALU.mult))

            def stats_x(u, n, loaded):
                dve.wait_ge(kx_loaded[u], loaded)
                for half in range(2):
                    ins = nc.vector.bn_stats(bn[u][:, half, :], x_in[u][:, half * 512:(half + 1) * 512])
                ins.then_inc(stats_ready, 1)
                dve.wait_ge(stats_ready, n)
                apart(dve)
                nc.vector.bn_aggr(mv[u][:, :], bn[u][:, :, :].rearrange("p a b -> p (a b)")).then_inc(var_ready, 1)

            def norm_x(u, col, n):
                dve.wait_ge(rstd_ready, n)
                nc.vector.tensor_copy(rstd_t[:, ds(col, 1)], rstd[u][:, :])
                nc.vector.tensor_scalar(x_in[u], x_in[u], mv[u][:, 0:1], rstd[u][:, :],
                                        ALU.subtract, ALU.mult).then_inc(kx_ready, 1)

            def low_x(u, n):
                dve.wait_ge(kxhi_ready, n)
                nc.vector.scalar_tensor_tensor(x_hl[u][:, LO, :], x_in[u], XS, x_hl[u][:, HI, :],
                                               ALU.mult, ALU.subtract).then_inc(kxlo_ready, 1)

            def low_wkv(q):
                dve.wait_ge(wkv_hi, q + 1)
                nc.vector.scalar_tensor_tensor(wkv[:, q, LO, :], kv_stage[q], WS, wkv[:, q, HI, :],
                                               ALU.mult, ALU.subtract).then_inc(wkv_ready, 1)

            for b in range(TOKEN_BLOCKS):
                u, tb = b % 2, slice(b * (BLOCK // P), (b + 1) * (BLOCK // P))
                whole = (P, BLOCK // P, EXPERTS)
                dve.wait_ge(logits_done, b + 1)
                own.link(nc.vector.tensor_copy(sums_x[:, tb, :], by_token(u)))
                nc.vector.tensor_tensor(logits[:, tb, :], sums_x[:, tb, EXPERTS:EXPERTS + 1].to_broadcast(whole),
                                        rw_sum[:, :].unsqueeze(1).to_broadcast(whole), ALU.mult).then_inc(logits_read, 1)
                dve.wait_ge(logits_read, b + 3)
                own.link(nc.vector.tensor_tensor(logits[:, tb, :], logits[:, tb, :], sums_x[:, tb, 0:EXPERTS], ALU.add))
                for t in range(tb.start, tb.stop):
                    ins = nc.vector.max(top_v[:, t, :], logits[:, t, :])
                own.link(ins)
                for t in range(tb.start, tb.stop):
                    ins = nc.vector.max_index(top_i[:, t, :], top_v[:, t, :], logits[:, t, :])
                own.link(ins)
                own.link(nc.vector.tensor_copy(top_f[:, :, tb].rearrange("p k t -> p t k"), top_i[:, tb, 0:TOPK]))
                for k in range(TOPK):
                    ins = nc.vector.tensor_tensor(
                        chosen[:, k, :, tb], top_f[:, k, tb].unsqueeze(1).to_broadcast((P, EXPERTS, BLOCK // P)),
                        iota[:, 0:EXPERTS].unsqueeze(2).to_broadcast((P, EXPERTS, BLOCK // P)), ALU.is_equal)
                ins.then_inc(chosen_ready, 1)
                if b < EARLY:
                    low_wkv(b)
                if b == 1:
                    for u in range(2):
                        stats_x(u, u + 1, 16)
                    for u in range(2):
                        norm_x(u, u, u + 1)

            def flat4(a):
                return a[:, :, :, :].rearrange("p k e t -> p (k e t)")

            dve.wait_ge(places_ready, 1)
            own.link(nc.vector.tensor_copy(flat4(totals), out_bank(1)))
            own.link(nc.vector.tensor_tensor_scan(flat4(running), run_mask[:, :, :].rearrange("p a t -> p (a t)"),
                                                  flat4(totals), 0.0, ALU.mult, ALU.add))
            own.link(nc.vector.tensor_tensor(flat4(place), flat4(running), flat4(totals), ALU.subtract))
            own.link(nc.vector.tensor_tensor(flat4(place), flat4(place), out_bank(0), ALU.add))
            for e in range(EXPERTS):
                ins = nc.vector.tensor_scalar(place[:, 1, e, :], place[:, 1, e, :], running[:, 0, e, TILES - 1:TILES],
                                              None, ALU.add)
            own.link(ins)
            own.link(nc.vector.scalar_tensor_tensor(flat4(place), flat4(place), float(CAPACITY), flat4(chosen),
                                                    ALU.is_lt, ALU.mult))
            own.link(nc.vector.tensor_reduce(keep[:, :, :], place[:, :, :, :].rearrange("p k e t -> p k t e"),
                                             AX.X, ALU.add))
            kept = small[:, 1, :]
            own.link(nc.vector.tensor_tensor(kept, keep[:, 0, :], keep[:, 1, :], ALU.max))
            nc.vector.tensor_copy(kept_h[:, :], kept).then_inc(kept_ready, 1)
            for k in range(TOPK):
                nc.vector.tensor_tensor(prob[:, k, :], top_v[:, :, k], top_v[:, :, 0], ALU.subtract)
            nc.vector.tensor_tensor(logits[:, :, :], logits[:, :, :],
                                    top_v[:, :, 0:1].to_broadcast((P, TILES, EXPERTS)), ALU.subtract)
            dve.wait_ge(ranks_ready, 1)
            tile_kept, run_kept, start = small[:, 2, :], small[:, 3, :], small[:, 4, :]
            nc.vector.tensor_copy(tile_kept, bank[1][:, 0:TILES])
            own.link(nc.vector.tensor_copy(rank[:, 0:TILES], bank[0][:, 0:TILES]))
            own.link(nc.vector.scalar_tensor_tensor(rank_kept[:, 0:TILES], rank[:, 0:TILES], 1.0, kept,
                                                    ALU.add, ALU.mult))
            own.link(nc.vector.tensor_scalar(rank_kept[:, 0:TILES], rank_kept[:, 0:TILES], -1.0, None, ALU.add))

            def kept_columns(u, col):
                return nc.vector.tensor_scalar(select[u][:, 1, :], iota[:, :], rank_kept[:, ds(col, 1)], None,
                                               ALU.is_equal)

            kept_columns(0, 0).then_inc(select_ready, 1)
            low_x(0, 1)
            own.link(nc.vector.tensor_tensor_scan(run_kept, run_mask[:, 0, :], tile_kept, 0.0, ALU.mult, ALU.add))
            own.link(nc.vector.tensor_tensor(start, run_kept, tile_kept, ALU.subtract))
            nc.vector.memset(start_i[:, 0:1], 0)
            nc.vector.tensor_copy(start_i[:, 1:TILES + 1], start)
            nc.vector.tensor_copy(start_i[:, TILES + 1:TILES + 2], run_kept[:, TILES - 1:TILES])
            own.link(nc.vector.tensor_tensor(start, start, rank[:, 0:TILES], ALU.add))
            own.link(nc.vector.scalar_tensor_tensor(start, start, -float(NO_ROW), kept, ALU.add, ALU.mult))
            own.link(nc.vector.tensor_scalar(start, start, float(NO_ROW), None, ALU.add))
            nc.vector.tensor_copy(slot_i[:, :], start)
            last_tile, count = small[:, 5, :], small[:, 6, :]
            own.link(nc.vector.scalar_tensor_tensor(last_tile, tile_kept, 0.0, iota[:, 1:TILES + 1],
                                                    ALU.is_gt, ALU.mult))
            own.link(nc.vector.tensor_reduce(loops_f[:, 0:1], last_tile, AX.X, ALU.max))
            own.link(nc.vector.tensor_scalar(count[:, 0:TILES // 2], iota[:, 0:TILES // 2], 2.0, loops_f[:, 0:1],
                                             ALU.mult, ALU.is_lt))
            own.link(nc.vector.tensor_reduce(loops_f[:, 0:1], count[:, 0:TILES // 2], AX.X, ALU.add))
            tail_starts = iota[:, 0:SLOT_TILES + 1]
            own.link(nc.vector.tensor_scalar(loops_f[:, 1:2], run_kept[:, TILES - 1:TILES], -1.0, float(SLOTS),
                                             ALU.mult, ALU.add))
            own.link(nc.vector.tensor_scalar(count[:, 0:SLOT_TILES + 1], tail_starts, float(P), loops_f[:, 1:2],
                                             ALU.mult, ALU.is_le))
            own.link(nc.vector.tensor_reduce(loops_f[:, 1:2], count[:, 0:SLOT_TILES + 1], AX.X, ALU.add))
            own.link(nc.vector.tensor_copy(loops_i[:, :], loops_f[:, :]))

            nc.vector.memset(carry[:, :], 0.0).then_inc(win_ready, 1)
            nc.vector.memset(upto[1][:, :], 0.0)
            kept_columns(1, 1)
            nc.vector.memset(scratch[30], 0.0).then_inc(tables_ready, 1)

            for s in (1, 3):
                dve.wait_ge(stage_done, s + 1)
                read_selected(nc.vector.tensor_copy, 0, s, FIRST_PAIRS[s], slice(0, P), stage_dve)
            for q in range(EARLY, CH):
                low_wkv(q)
            low_x(1, 2)
            for q in range(CH, 2 * CH):
                low_wkv(q)
            dve.wait_ge(wkv_ready, 2 * CH)
            dve.wait_ge(rows_loaded, 48)
            pairs = dve.value_load(loops_i[0:1, 0:1], min_val=1, max_val=TILES // 2)

            def sums(u, t, n):
                dve.wait_ge(stage_done, n + 1)
                dve.wait_ge(win_stored, 16 * t + 16)
                dve.wait_ge(win_ready, t + 1)
                w = window[u]
                for c in range(2):
                    ins = nc.vector.scalar_tensor_tensor(
                        w[:, 4 * c:4 * c + 4, :],
                        bank[2 + u][:, c * BLOCK:(c + 1) * BLOCK].rearrange("p (c s) -> p c s", c=4), 1.0 / KVS,
                        carry[:, 4 * c:4 * c + 4].unsqueeze(2).to_broadcast((P, 4, P)), ALU.mult, ALU.add)
                ins.then_inc(stage_dve, 1)
                dve.wait_ge(stage_dve, 3 * t + 3)
                nc.vector.tensor_scalar(carry[:, :], w[:, :, P - 1], go_on[:, ds(t, 1)], None, ALU.mult)\
                  .then_inc(win_ready, 1)

            with dve.Fori(0, pairs) as g:
                for u in range(2):
                    t = 2 * g + u
                    e = [slice(h * BLOCK, (h + 1) * BLOCK) for h in range(2)]

                    def read_k(half):
                        dve.wait_ge(proj_done, 4 * t + half + 1)
                        nc.vector.scalar_tensor_tensor(k_raw[:, e[half]], out_bank(half), INV_XW, bk_row[:, e[half]],
                                                       ALU.mult, ALU.add).then_inc(proj_read, 1)

                    read_k(0)
                    sums(u, t, 5 * t + 4)
                    at = dve.value_load(start_i[0:1, ds(t + 2, 1)], min_val=0, max_val=SLOTS)

                    def read_odd(s):
                        dve.wait_ge(stage_done, 5 * t + 4 + 1 + s + 1)
                        read_selected(nc.vector.tensor_copy, 1 - u, s, 2 + (u + 1 + s) % 2, ds(at, P), stage_dve)

                    stats_x(u, t + 3, 16 * g + 32)
                    read_k(1)
                    read_odd(1)
                    norm_x(u, t + 2, t + 3)
                    kept_columns(u, t + 2)
                    nc.vector.tensor_scalar(upto[u][:, :], iota[:, :], rank[:, ds(t, 1)], None, ALU.is_ge)
                    for half in range(2):
                        dve.wait_ge(kexp_ready, 2 * t + half + 1)
                        ins = nc.vector.scalar_tensor_tensor(k_exp[:, e[half]], k_exp[:, e[half]], 1.0,
                                                             k_raw[:, e[half]], ALU.min, ALU.add)
                        ins.then_inc(phik_ready, 1)
                    low_x(u, t + 3)
                    for half in range(2):
                        dve.wait_ge(proj_done, 4 * t + 2 + half + 1)
                        nc.vector.scalar_tensor_tensor(v_raw[:, e[half]], out_bank(2 + half), INV_XW,
                                                       bv_row[:, e[half]], ALU.mult, ALU.add)\
                          .then_inc(proj_read, 1)
                        dve.wait_ge(proj_read, 4 + 4 * t + 2 + half + 1)
                        dve.wait_ge(phik_ready, 2 * t + half + 1)
                        nc.vector.tensor_tensor(v_raw[:, e[half]], v_raw[:, e[half]], k_exp[:, e[half]], ALU.mult)\
                          .then_inc(kv_ready, 1)
                        if half == 0:
                            read_odd(3)
                    for half in range(2):
                        dve.wait_ge(kvhi_ready, 2 * t + half + 1)
                        ins = nc.vector.scalar_tensor_tensor(kv_hl[:, LO, e[half]], v_raw[:, e[half]], KVS,
                                                             kv_hl[:, HI, e[half]], ALU.mult, ALU.subtract)
                        ins.then_inc(kvlo_ready, 1)
            kept = dve.value_load(start_i[0:1, TILES + 1:TILES + 2], min_val=0, max_val=SLOTS)
            tails = dve.value_load(loops_i[0:1, 1:2], min_val=1, max_val=SLOT_TILES + 1)
            with dve.Fori(0, tails) as n:
                at = nc.s_assert_within(kept + n * P, 0, SLOTS)
                nc.vector.tensor_copy(xnT[:, :, :, :].rearrange("p h c s -> p (h c) s")[:, :, ds(at, P)],
                                      zero_c[:, :].unsqueeze(2).to_broadcast((P, 2 * CH, P)))

            def piece_lo(grp, par, q):
                dve.wait_ge(whi_ready, PIECES * grp + q + 1)
                nc.vector.scalar_tensor_tensor(ring[par][:, q, LO, :], stage[q % 2][:, :], WS, ring[par][:, q, HI, :],
                                               ALU.mult, ALU.subtract).then_inc(wlo_ready, 1)

            for q in range(2):
                piece_lo(0, 0, q)
            last = 2 * pairs
            sums(0, last, 10 * pairs + 4)
            nc.vector.memset(scratch[31], 0.0).then_inc(sums_done, 1)

            for q in range(2, PIECES):
                piece_lo(0, 0, q)
            own = Chain(dve, dve_weights)
            nc.vector.tensor_tensor(prob[:, :, :], prob[:, :, :],
                                    rstd_t[:, 0:TILES].unsqueeze(1).to_broadcast((P, TOPK, TILES)), ALU.mult)
            nc.vector.tensor_tensor(logits[:, :, :], logits[:, :, :],
                                    rstd_t[:, 0:TILES].unsqueeze(2).to_broadcast((P, TILES, EXPERTS)), ALU.mult)\
              .then_inc(scaled, 1)
            dve.wait_ge(probs_ready, 1)
            own.link(nc.vector.tensor_reduce(z[:, :], logits[:, :, :], AX.X, ALU.add))
            own.link(nc.vector.reciprocal(z[:, :], z[:, :]))
            own.link(nc.vector.tensor_tensor(prob[:, :, :], prob[:, :, :], keep[:, :, :], ALU.mult))
            own.link(nc.vector.tensor_tensor(prob[:, 0, :], prob[:, 0, :], prob[:, 1, :], ALU.add))
            nc.vector.tensor_tensor(meta[:, :, 1].bitcast(F32), prob[:, 0, :], z[:, :], ALU.mult).then_inc(meta_ready, 1)

            def phi_q(s, f):
                dve.wait_ge(up_read, 4 + FT * s + f + 1)
                nc.vector.scalar_tensor_tensor(h_f32[f], q_exp[f], 1.0, h_f32[f], ALU.min, ALU.add).then_inc(phi_ready, 1)

            def context(s, f):
                dve.wait_ge(phi_ready, FT * s + f + 1)
                dve.wait_ge(kvq_loaded[f], 16 * s + 16)
                nc.vector.scalar_tensor_tensor(h_f32[f], h_f32[f], SCALE * CS, kvq[f], ALU.mult, ALU.mult)\
                  .then_inc(ctx_ready, 1)

            def low_h(s, j, f, factor):
                dve.wait_ge(hhi_ready, FT * s + f + 1)
                nc.vector.scalar_tensor_tensor(h_hl[j % 2][:, f, LO, :], h_f32[f], factor,
                                               h_hl[j % 2][:, f, HI, :], ALU.mult, ALU.subtract).then_inc(hlo_ready, 1)

            def add_down(s, j, m, factor, start_count):
                dve.wait_ge(acc_ready, start_count)
                dve.wait_ge(down_done, 16 + 8 * s + m + 1)
                row = acc[:, 4 * (j % BLOCKS) + m // 2, (m % 2) * BLOCK:(m % 2 + 1) * BLOCK]
                nc.vector.scalar_tensor_tensor(row, out_bank(4 + m % 4), factor, row, ALU.mult, ALU.add)\
                  .then_inc(down_added, 1)

            def result(st):
                dve.wait_ge(g_ready, st + 1)
                dve.wait_ge(fs_loaded[st % FS], 16 * (st // FS + 1))
                nc.vector.tensor_tensor(fs[st % FS], fs[st % FS], fg[st % 2], ALU.mult).then_inc(fin_ready, 1)

            def attention_body(base_group):
                n = 2 * BLOCKS
                for j in range(n + 1):
                    s = BLOCKS * base_group + j
                    grp = base_group + j // BLOCKS

                    def added(m):
                        if j >= 1:
                            add_down(s - 1, j - 1, m, 1.0 / (CS * WS), (j - 1) % BLOCKS + 1)

                    if j < n:
                        phi_q(s, 0)
                        context(s, 0)
                        phi_q(s, 1)
                    added(0)
                    if j < n:
                        context(s, 1)
                        low_h(s, j, 0, 1.0)
                    added(1)
                    if j < n:
                        low_h(s, j, 1, 1.0)
                    added(2)
                    if j < n:
                        piece_lo(grp + 1, 1 - j // BLOCKS, j % BLOCKS)
                    for m in range(3, 8):
                        added(m)

            def ffn_body(base_group, last=False):
                n = 2 * BLOCKS
                for j in range(n + 1):
                    s = BLOCKS * base_group + j
                    if j < n:
                        for f in range(FT):
                            low_h(s, j, f, HS)
                        if not (last and j >= BLOCKS):
                            piece_lo(base_group + j // BLOCKS + 1, 1 - j // BLOCKS, j % BLOCKS)
                    if j >= 1:
                        b = (j - 1) % BLOCKS
                        tile = (BLOCK // P) * b
                        gated = last and j > BLOCKS
                        for m in range(8):
                            add_down(s - 1, j - 1, m, 1.0 / (HS * WS), BLOCKS + b + 1)
                            if gated and m % 2 and m >= 3:
                                result(tile + m // 2 - 1)
                        if gated:
                            result(tile + BLOCK // P - 1)

            with dve.Fori(0, ATT_GROUPS // 2) as g:
                attention_body(2 * g)
            with dve.Fori(0, FFN_GROUPS // 2 - 1) as g:
                ffn_body(ATT_GROUPS + 2 * g)
            ffn_body(GROUPS - 2, last=True)

        @block.tensor
        def _(pe):
            mm = nc.tensor.matmul
            pe.wait_ge(const_ready, 1)
            pe.wait_ge(router_loaded, 16)

            for c in range(CH):
                ins = mm(bank[3][:, 0:EXPERTS], ones_f, rw_f[:, c, 0:EXPERTS], start=(c == 0), stop=(c == CH - 1))
            ins.then_inc(sums_w_done, 1)
            pe.wait_ge(ident_ready, 1)
            def scores_by_expert(u, loaded, chunks):
                pe.wait_ge(xt_loaded[u], 16 * loaded)
                for c in chunks:
                    ins = mm(scores(u), rw_f[:, c, :], xt_in[u][:, c, :], start=(c == 0), stop=(c == CH - 1))
                return ins

            def scores_by_token(u, b):
                pe.wait_ge(scores_read, b + 1)
                pe.wait_ge(logits_read, b + 1)
                for i in range(BLOCK // P):
                    ins = mm(by_token(u)[:, i, :],
                             by_expert[u][0:EXPERTS + 1, i * P:(i + 1) * P], ident_f[0:EXPERTS + 1, :],
                             start=True, stop=True)
                ins.then_inc(logits_done, 1)

            def block_scores(u, b, loaded):
                scores_by_expert(u, loaded, range(CH // 4))
                scores_by_token(1 - u, b - 1)
                scores_by_expert(u, loaded, range(CH // 4, CH)).then_inc(scores_done, 1)

            scores_by_expert(0, 1, range(CH)).then_inc(scores_done, 1)
            with pe.Fori(0, TOKEN_BLOCKS // 2 - 1) as g:
                block_scores(1, 2 * g + 1, g + 1)
                block_scores(0, 2 * g + 2, g + 2)
            block_scores(1, TOKEN_BLOCKS - 1, TOKEN_BLOCKS // 2)
            scores_by_token(1, TOKEN_BLOCKS - 1)

            pe.wait_ge(chosen_ready, TOKEN_BLOCKS)
            picks = chosen[:, :, :, :].rearrange("p k e t -> p (k e t)")
            mm(out_bank(0), before[:, :], picks, start=True, stop=True)
            mm(out_bank(1), ones[:, :], picks, start=True, stop=True).then_inc(places_ready, 1)
            pe.wait_ge(kept_ready, 1)
            mm(bank[0][:, 0:TILES], before[:, :], kept_h[:, :], start=True, stop=True)
            mm(bank[1][:, 0:TILES], ones[:, :], kept_h[:, :], start=True, stop=True).then_inc(ranks_ready, 1)

            def select_x(u, s, pair):
                for c in range(4):
                    cc = 4 * (s % 2) + c
                    ins = mm(bank[pair][:, c * 2 * P:(c + 1) * 2 * P], x_hl[u][:, s // 2, cc * P:(cc + 1) * P],
                             select[u][:, :, :].rearrange("p w t -> p (w t)"), start=True, stop=True)
                ins.then_inc(stage_done, 1)

            pe.wait_ge(select_ready, 1)
            pe.wait_ge(kxhi_ready, 1)
            for s in range(4):
                if s == 2:
                    pe.wait_ge(kxlo_ready, 1)
                select_x(0, s, FIRST_PAIRS[s])
            pe.wait_ge(wkv_ready, EARLY)
            pe.wait_ge(tables_ready, 1)
            pairs = pe.value_load(loops_i[0:1, 0:1], min_val=1, max_val=TILES // 2)

            def project(u, t, n):
                pe.wait_ge(proj_read, 4 * t + n + 1)
                e = slice((n % 2) * BLOCK, (n % 2 + 1) * BLOCK)
                k = 0
                for c in range(CH):
                    if n == 0 and c == EARLY:
                        pe.wait_ge(wkv_ready, CH)
                    for a, b in PASSES:
                        ins = mm(out_bank(n), xT[u][:, a, c, :], wkv[:, (n // 2) * CH + c, b, e],
                                 start=(k == 0), stop=(k == 3 * CH - 1))
                        k += 1
                ins.then_inc(proj_done, 1)

            def sum_kv(u, par, n):
                for c in range(CH):
                    for h in (HI, LO):
                        ins = mm(bank[2 + u][:, c * P:(c + 1) * P], kv_hl[:, h, c * P:(c + 1) * P], upto[par][:, :],
                                 start=(h == HI), stop=(h == LO))
                ins.then_inc(stage_done, 1)

            with pe.Fori(0, pairs) as g:
                for u in range(2):
                    t = 2 * g + u
                    pe.wait_ge(stage_act, 2 * t + 2)
                    pe.wait_ge(stage_dve, 3 * t + 2)
                    project(u, t, 0)
                    pe.wait_ge(kvlo_ready, 2 * t + 2)
                    sum_kv(u, 1 - u, 5 * t + 4)
                    pe.wait_ge(kxlo_ready, t + 2)
                    for s in range(4):
                        if s == 1:
                            project(u, t, 1)
                            pe.wait_ge(stage_dve, 3 * t + 3)
                        if s == 2:
                            pe.wait_ge(stage_act, 2 * t + 3)
                        if s == 3:
                            pe.wait_ge(wkv_ready, 2 * CH)
                            project(u, t, 2)
                            pe.wait_ge(stage_dve, 3 * t + 4)
                        select_x(1 - u, s, 2 + (u + 1 + s) % 2)
                    project(u, t, 3)
            pe.wait_ge(kvlo_ready, 4 * pairs + 2)
            pe.wait_ge(stage_dve, 6 * pairs + 2)
            pe.wait_ge(stage_act, 4 * pairs + 2)
            sum_kv(0, 1, 10 * pairs + 4)

            def up(s, j, grp, par):
                pe.wait_ge(wlo_ready, PIECES * grp + 2)
                for f in range(FT):
                    pe.wait_ge(up_read, FT * s + f + 1)
                    k = 0
                    for c in range(CH):
                        w = ring[par][:, c // 4, :, :].rearrange("p h (c n) -> p h c n", c=4)
                        for a, b in PASSES:
                            ins = mm(out_bank(FT * (j % 2) + f), w[:, a, c % 4, f * P:(f + 1) * P],
                                     xnT[:, b, c, (j % BLOCKS) * BLOCK:(j % BLOCKS + 1) * BLOCK],
                                     start=(k == 0), stop=(k == 3 * CH - 1))
                            k += 1
                    ins.then_inc(up_done, 1)

            def down(s, j, grp, par):
                pe.wait_ge(wlo_ready, PIECES * grp + PIECES)
                pe.wait_ge(hlo_ready, FT * s + FT + FT)
                for m in range(8):
                    pe.wait_ge(down_added, 8 * s + m + 1)
                    k = 0
                    for f in range(FT):
                        for a, b in PASSES:
                            ins = mm(out_bank(4 + m % 4), h_hl[j % 2][:, f, a, (m // 2) * P:(m // 2 + 1) * P],
                                     ring[par][:, 2 + f, b, (m % 2) * BLOCK:(m % 2 + 1) * BLOCK],
                                     start=(k == 0), stop=(k == 3 * FT - 1))
                            k += 1
                    ins.then_inc(down_done, 1)

            def body(base_group):
                n = 2 * BLOCKS
                for j in range(n + 1):
                    if j < n:
                        up(BLOCKS * base_group + j, j, base_group + j // BLOCKS, j // BLOCKS)
                    if j >= 1:
                        down(BLOCKS * base_group + j - 1, j - 1, base_group + (j - 1) // BLOCKS, (j - 1) // BLOCKS)

            with pe.Fori(0, GROUPS // 2) as g:
                body(2 * g)


_OUTS = [((4, 1024, 1024), "float32")]


def kernel(L0_attn_x, L0_attn_Wq, L0_attn_bq, L0_attn_Wk, L0_attn_bk, L0_attn_Wv, L0_attn_bv, L0_attn_Wo,
           L0_attn_bo, L0_ffn_router_w, L0_ffn_w1, L0_ffn_b1, L0_ffn_w2, L0_ffn_b2):
    import concourse.bacc as bacc
    from concourse.bass_utils import run_bass_kernel_spmd

    def rows_in(w):
        return np.asarray(w).T.reshape(-1, P, w.shape[0])

    def groups(up, down, n):
        a = rows_in(up).reshape(CH, P, n, GF).transpose(2, 1, 0, 3).reshape(n, P, 2, 1024)
        b = rows_in(down).reshape(n, FT, P, D).transpose(0, 2, 1, 3)
        return np.concatenate([a, b], axis=2)

    def columns(b):
        return np.asarray(b).reshape(-1, P).T

    arrays = {
        "x": np.asarray(L0_attn_x).reshape(TOKENS, D),
        "x_t": np.asarray(L0_attn_x).reshape(TOKEN_BLOCKS, BLOCK, CH, P).transpose(0, 3, 2, 1),
        "w_kv": np.concatenate([rows_in(L0_attn_Wk), rows_in(L0_attn_Wv)]),
        "router": rows_in(L0_ffn_router_w).transpose(1, 0, 2),
        "w_groups": np.concatenate([groups(L0_attn_Wq, L0_attn_Wo, ATT_GROUPS),
                                    groups(L0_ffn_w1, L0_ffn_w2, FFN_GROUPS)]),
        "b_k": np.asarray(L0_attn_bk).reshape(1, D), "b_v": np.asarray(L0_attn_bv).reshape(1, D),
        "b_q": columns(L0_attn_bq), "b_o": np.asarray(L0_attn_bo).reshape(1, D),
        "b_1": columns(L0_ffn_b1), "b_2": np.asarray(L0_ffn_b2).reshape(1, D),
    }
    arrays = {n: np.ascontiguousarray(a) for n, a in arrays.items()}
    nc = bacc.Bacc("TRN2", target_bir_lowering=False, num_devices=1)
    args = [nc.dram_tensor(n, a.shape, F32, kind="ExternalInput").ap() for n, a in arrays.items()]
    out = nc.dram_tensor("out", (TOKENS, D), F32, kind="ExternalOutput").ap()
    build(nc, *args, out)
    r = run_bass_kernel_spmd(nc, [arrays], core_ids=[0])
    return r.results[0]["out"].reshape(4, 1024, 1024)
```
